# Optimizing a Trainium2 kernel written in Bass

```python
import numpy as np
import jax
import jax.numpy as jnp

def _softmax(x, axis=-1):
    return jax.nn.softmax(x, axis=axis)

def _gelu(x):
    return jax.nn.gelu(x, approximate=True)

def _silu(x):
    return jax.nn.silu(x)

def _sigmoid(x):
    return jax.nn.sigmoid(x)

def _layernorm(x, axis=-1, eps=1e-05):
    m = jnp.mean(x, axis=axis, keepdims=True)
    v = jnp.var(x, axis=axis, keepdims=True)
    return (x - m) / jnp.sqrt(v + eps)

def _scatter_add(tgt, idx, src, axis=0):
    return tgt.at[idx].add(src)

def _segment_sum(src, seg, n):
    return jax.ops.segment_sum(src, seg, n)
kernel_name = 'mk_macaron_d1_jaxref_r8_1f7e15'

def setup_inputs(seed: int=0):
    np.random.seed(seed)
    _w = jnp.asarray

    def _L0_attn_setup():
        import jax, jax.numpy as jnp
        import numpy as np
        from math import log2, floor
        HEADS = 16
        DIM_HEAD = 64
        SCALE = DIM_HEAD ** (-0.5)

        def _get_slopes(heads):

            def pow2_slopes(n):
                start = 2 ** (-2 ** (-(log2(n) - 3)))
                return [start * start ** i for i in range(n)]
            if log2(heads).is_integer():
                return pow2_slopes(heads)
            c = 2 ** floor(log2(heads))
            return pow2_slopes(c) + pow2_slopes(2 * c)[0::2][:heads - c]
        key = jax.random.key(seed)
        k1, k2, k3 = jax.random.split(key, 3)
        b, n, dim = (2, 256, 128)
        inner = HEADS * DIM_HEAD
        x = jax.random.normal(k1, (b, n, dim), dtype=jnp.float32)
        w_qkv = jax.random.normal(k2, (dim, 3 * inner), dtype=jnp.float32) * dim ** (-0.5)
        w_out = jax.random.normal(k3, (inner, dim), dtype=jnp.float32) * inner ** (-0.5)
        b_out = jnp.zeros((dim,), dtype=jnp.float32)
        return {'x': x, 'w_qkv': w_qkv, 'w_out': w_out, 'b_out': b_out}
    _L0_attn_in = _L0_attn_setup()

    def _L0_ffn_setup():
        import jax, jax.numpy as jnp
        import numpy as np
        import math
        BETA = 0.9
        THRESHOLD = 1.0
        NUM_STEPS = 5
        ALPHA = 2.0

        @jax.custom_vjp
        def spike_fn(u):
            return (u > 0).astype(u.dtype)

        def _spike_fwd(u):
            return (spike_fn(u), u)

        def _spike_bwd(u, g):
            s = jnp.pi / 2.0 * ALPHA * u
            return (g * (ALPHA / 2.0) / (1.0 + s * s),)
        spike_fn.defvjp(_spike_fwd, _spike_bwd)
        key = jax.random.key(seed)
        k1, k2, k3 = jax.random.split(key, 3)
        n_embd = 128
        x = jax.random.normal(k1, (4, 256, n_embd), dtype=jnp.float32)
        W_fc = jax.random.normal(k2, (4 * n_embd, n_embd), dtype=jnp.float32) / math.sqrt(n_embd)
        W_proj = jax.random.normal(k3, (n_embd, 4 * n_embd), dtype=jnp.float32) / math.sqrt(4 * n_embd)
        return {'x': x, 'W_fc': W_fc, 'W_proj': W_proj}
    _L0_ffn_in = _L0_ffn_setup()
    _d = {'L0_attn_x': _L0_attn_in['x'], 'L0_attn_w_qkv': _L0_attn_in['w_qkv'], 'L0_attn_w_out': _L0_attn_in['w_out'], 'L0_attn_b_out': _L0_attn_in['b_out'], 'L0_ffn_W_fc': _L0_ffn_in['W_fc'], 'L0_ffn_W_proj': _L0_ffn_in['W_proj']}
    _x0 = _d['L0_attn_x']
    _d['L0_attn_x'] = jax.random.normal(jax.random.fold_in(jax.random.key(seed), 1), (16, 512, 128), dtype=_x0.dtype)
    del _x0
    return _d

def reference(L0_attn_x, L0_attn_w_qkv, L0_attn_w_out, L0_attn_b_out, L0_ffn_W_fc, L0_ffn_W_proj):

    def _L0_attn_ref(x, w_qkv, w_out, b_out):
        import jax, jax.numpy as jnp
        import numpy as np
        from math import log2, floor
        HEADS = 16
        DIM_HEAD = 64
        SCALE = DIM_HEAD ** (-0.5)

        def _get_slopes(heads):

            def pow2_slopes(n):
                start = 2 ** (-2 ** (-(log2(n) - 3)))
                return [start * start ** i for i in range(n)]
            if log2(heads).is_integer():
                return pow2_slopes(heads)
            c = 2 ** floor(log2(heads))
            return pow2_slopes(c) + pow2_slopes(2 * c)[0::2][:heads - c]
        b, n, _ = x.shape
        qkv = x @ w_qkv
        q, k, v = jnp.split(qkv, 3, axis=-1)

        def to_heads(t):
            return t.reshape(b, n, HEADS, DIM_HEAD).transpose(0, 2, 1, 3)
        q, k, v = map(to_heads, (q, k, v))
        q = q * SCALE
        sim = jnp.einsum('bhid,bhjd->bhij', q, k)
        slopes = jnp.asarray(_get_slopes(HEADS), dtype=sim.dtype)[:, None, None]
        i = jnp.arange(n)
        rel = -jnp.abs(i[None, :] - i[:, None]).astype(sim.dtype)
        sim = sim + rel[None, :, :] * slopes
        causal = jnp.triu(jnp.ones((n, n), dtype=bool), 1)
        mask_value = -jnp.finfo(sim.dtype).max
        sim = jnp.where(causal, mask_value, sim)
        attn = jax.nn.softmax(sim, axis=-1)
        out = jnp.einsum('bhij,bhjd->bhid', attn, v)
        out = out.transpose(0, 2, 1, 3).reshape(b, n, HEADS * DIM_HEAD)
        return out @ w_out + b_out

    def _L0_ffn_ref(x, W_fc, W_proj):
        import jax, jax.numpy as jnp
        import numpy as np
        import math
        BETA = 0.9
        THRESHOLD = 1.0
        NUM_STEPS = 5
        ALPHA = 2.0

        @jax.custom_vjp
        def spike_fn(u):
            return (u > 0).astype(u.dtype)

        def _spike_fwd(u):
            return (spike_fn(u), u)

        def _spike_bwd(u, g):
            s = jnp.pi / 2.0 * ALPHA * u
            return (g * (ALPHA / 2.0) / (1.0 + s * s),)
        spike_fn.defvjp(_spike_fwd, _spike_bwd)
        h = jnp.square(jax.nn.relu(jnp.einsum('bsd,fd->bsf', x, W_fc)))
        y = jnp.einsum('bsf,df->bsd', h, W_proj)

        def step(mem, _):
            reset = jax.lax.stop_gradient(spike_fn(mem - THRESHOLD))
            mem_new = BETA * mem + y - reset * THRESHOLD
            spk = spike_fn(mem_new - THRESHOLD)
            return (mem_new, spk)
        mem0 = jnp.zeros_like(y)
        _, spks = jax.lax.scan(step, mem0, None, length=NUM_STEPS)
        return jnp.sum(spks, axis=0) / NUM_STEPS
    x = L0_attn_x
    x = x + 0.5 * _L0_ffn_ref(_layernorm(x, axis=-1), L0_ffn_W_fc, L0_ffn_W_proj)
    x = x + _L0_attn_ref(_layernorm(x, axis=-1), L0_attn_w_qkv, L0_attn_w_out, L0_attn_b_out)
    x = x + 0.5 * _L0_ffn_ref(_layernorm(x, axis=-1), L0_ffn_W_fc, L0_ffn_W_proj)
    return x

_drawn_inputs = setup_inputs


def setup_inputs(seed=0):
    import zlib

    import numpy as np

    out = dict(_drawn_inputs(seed))
    spreads = {'L0_attn_b_out': (0.0, 0.1)}
    factors = {}
    for name, (base, spread) in spreads.items():
        noise = np.random.default_rng([zlib.crc32(name.encode()), seed]).standard_normal(out[name].shape)
        drawn = base * np.exp(spread * noise) if base else spread * noise
        out[name] = jnp.asarray(drawn.astype(out[name].dtype))
    for name, factor in factors.items():
        out[name] = (out[name] * factor).astype(out[name].dtype)
    return out
```

```python
from contextlib import ExitStack

import concourse.bass as bass
from concourse import mybir

ALU = mybir.AluOpType
ACT = mybir.ActivationFunctionType
F32 = mybir.dt.float32
F32R = mybir.dt.float32r

P = 128
B, N, C = 16, 512, 128
HEADS, DH = 16, 64
F = 4 * C
NT = N // P
FC = F // P
PAIRS = HEADS // 2
INNER = HEADS * DH
SCALE = DH ** -0.5
EPS = 1e-5
BETA, THRESHOLD, STEPS = 0.9, 1.0, 5
SLOPES = [2.0 ** (-0.5 * (h + 1)) for h in range(HEADS)]
MASKED = 3.0e38

TILES = [[(0, 3)], [(1, 3)], [(0, 2)], [(1, 2)], [(0, 1), (1, 1)], [(0, 0), (1, 0)]]
BEATS = len(TILES)
SEG = {hi: n for n, hi in enumerate(x for t in TILES for x in t)}
WIDTH = [(i + 1) * P for i in range(NT)]
PCOL = [sum(WIDTH[i + 1:]) for i in range(NT)]
PHEAD = sum(WIDTH)
TRUNS = [[(0, 0)], [(1, 0)], [(0, 1), (0, 3)], [(1, 1), (1, 3)], [(0, 2), (1, 2)]]
TBEAT = [2, 2, 3, 4, 5]
PVORDER = [0, 1, 3, 2]


def place_of(h, j):
    for t, runs in enumerate(TRUNS):
        col = 0
        for hh, jj in runs:
            if (hh, jj) == (h, j):
                return t, col
            col += (NT - jj) * P


SIDE = sorted(
    [(s, 3 + h, "g", h, 0 if s < PAIRS - 1 else 1) for s in range(PAIRS) for h in range(2)]
    + [(s, i, "v", i, 0) for s in range(1, PAIRS, 2) for i in range(2)]
    + [(1, 2, "t1", 0, 1), (2, 2, "fc1", 0, 1), (2, 3, "fc1", 1, 1), (3, 2, "fc1", 2, 1), (3, 3, "fc1", 3, 1),
       (4, 1, "y1", 0, 1), (7, 2, "t2", 0, 1)]
    + [(2, 0, "out", 0, -1), (4, 0, "t3", 0, -1), (4, 3, "fc3", 0, -1), (5, 2, "fc3", 1, -1),
       (5, 3, "fc3", 2, -1), (6, 0, "fc3", 3, -1), (6, 2, "y3", 0, -1)],
    key=lambda x: (x[0], x[1], x[2] == "g"))
assert len(SIDE) % 2 == 0


def macaron_kernel(nc: bass.Bass, x, w_qkv, w_out, b_out, w_fc, w_proj, out):
    ctx = ExitStack()
    with ctx:
        def sb(name, shape, dt=F32):
            return ctx.enter_context(nc.sbuf_tensor(name, shape, dt))

        def sem(name):
            return ctx.enter_context(nc.semaphore(name))

        banks = [ctx.enter_context(nc.psum_tensor(f"bank{i}", [P, 512], F32)) for i in range(8)]
        score_bank, turn_bank, pv_bank, side_bank = banks[0:3], banks[3:5], banks[5], banks[6:8]

        ident = sb("ident", [P, P])
        minus_half = sb("minus_half", [P, NT])
        eps = sb("eps", [P, NT])
        dist = sb("dist", [P, N])
        alibi = sb("alibi", [P, HEADS, N])
        a_hi = sb("a_hi", [P, HEADS, C], F32R)
        a_lo = sb("a_lo", [P, HEADS, C], F32R)
        wv_hi = sb("wv_hi", [P, INNER], F32R)
        wv_lo = sb("wv_lo", [P, INNER], F32R)
        wo = sb("wo", [P, PAIRS, C])
        wfc_hi = sb("wfc_hi", [P, F], F32R)
        wfc_lo = sb("wfc_lo", [P, F], F32R)
        wproj = sb("wproj", [P, FC, C])
        bias = sb("bias", [P, C])
        x_in = sb("x_in", [P, 2, NT, C])
        x1b = sb("x1b", [P, 2, NT, C])
        x1 = sb("x1", [P, NT, C])
        x2 = sb("x2", [P, NT, C])
        x3 = sb("x3", [P, NT, C])
        xn = sb("xn", [P, 3, NT, C])
        stats = sb("stats", [P, 3, NT, 6])
        meanvar = sb("meanvar", [P, 3, NT, 2])
        vareps = sb("vareps", [P, 3, NT])
        rstd = sb("rstd", [P, 3, NT])
        xf_hi = sb("xf_hi", [P, N], F32R)
        xf_lo = sb("xf_lo", [P, N], F32R)
        xa_hi = sb("xa_hi", [P, 2, N], F32R)
        xa_lo = sb("xa_lo", [P, 2, N], F32R)
        relu = sb("relu", [P, 2, N])
        hid = sb("hid", [P, FC, N])
        ysb = sb("ysb", [P, N])
        negmem = sb("negmem", [P, N])
        drive = sb("drive", [P, N])
        spikes = sb("spikes", [P, N])
        g_hi = sb("g_hi", [P, 2, 2, N], F32R)
        g_lo = sb("g_lo", [P, 2, 2, N], F32R)
        vals = sb("vals", [P, 2, NT, 4 * DH])
        negsc = sb("negsc", [P, 3, N])
        negmax = sb("negmax", [P, 2, 8])
        sums = sb("sums", [P, 2, 8])
        rsum = sb("rsum", [P, 2, 8])
        prob = sb("prob", [P, 2, 2, PHEAD])
        probT = sb("probT", [P, 2, len(TRUNS), N])
        attT = sb("attT", [P, PAIRS, N])
        w_raw = prob[:, :, :, :].rearrange("p a h n -> p (a h n)")[:, 0:3 * INNER]
        w_qkT = prob[:, :, :, :].rearrange("p a h n -> p (a h n)")[:, 3 * INNER:5 * INNER].rearrange(
            "p (t m c) -> p t m c", t=2, c=C)
        fc_raw, proj_raw = probT[:, 0, 0, :], probT[:, 0, 1, :]

        s_w, s_stored = sem("s_w"), sem("s_stored")
        s_xin = [sem("s_xin_even"), sem("s_xin_odd")]
        s_const, s_const0, s_dist0, s_wT, s_wTcopied = sem("s_const"), sem("s_const0"), sem("s_dist0"), sem("s_wT"), sem("s_wTcopied")
        s_a, s_acopied, s_split, s_alibi = sem("s_a"), sem("s_acopied"), sem("s_split"), sem("s_alibi")
        s_scores, s_biased, s_exp, s_rsum, s_norm = (sem(n) for n in ("s_scores", "s_biased", "s_exp", "s_rsum", "s_norm"))
        s_turned, s_turned_out, s_pv, s_att = (sem(n) for n in ("s_turned", "s_turned_out", "s_pv", "s_att"))
        s_g, s_ghi, s_glo, s_v, s_vals = (sem(n) for n in ("s_g", "s_ghi", "s_glo", "s_v", "s_vals"))
        s_fc, s_relu, s_hid, s_y, s_ysb, s_spk = (
            {w: sem(f"{n}{w}") for w in (1, 3)} for n in ("s_fc", "s_relu", "s_hid", "s_y", "s_ysb", "s_spk"))
        s_stats, s_mv, s_ve, s_rstd, s_xn, s_xT, s_xhi, s_xlo = (
            {w: sem(f"{n}{w}") for w in (1, 2, 3)}
            for n in ("s_stats", "s_mv", "s_ve", "s_rstd", "s_xn", "s_xT", "s_xhi", "s_xlo"))
        s_out, s_x1, s_x1b, s_x2, s_x3 = (sem(n) for n in ("s_out", "s_x1", "s_x1b", "s_x2", "s_x3"))

        def wait(eng, semaphore, value):
            if not isinstance(value, int) or value > 0:
                eng.wait_ge(semaphore, value)

        def tile_no(b, p, k):
            return b * (PAIRS * BEATS) + (p * BEATS + k + 1)

        def turn_no(b, p, t):
            return b * (PAIRS * len(TRUNS)) + (p * len(TRUNS) + t + 1)

        def pair_no(b, p):
            return b * PAIRS + (p + 1)

        def g_no(b, p, h):
            return b * HEADS + (2 * p + h + 1)

        def v_no(b, q, i):
            return b * PAIRS + (2 * q + i + 1)

        def before(b, p, back):
            return (b, p - back) if p >= back else (b - 1, p - back + PAIRS)

        def exists(b, p):
            return not isinstance(b, int) or (0 <= b < B)

        def freed(kind, i, b, s):
            if kind == "g":
                return s_glo, g_no(b, (s + 1) % PAIRS, i)
            if kind == "v":
                return s_vals, v_no(b, s // 2, i)
            if kind in ("t1", "t2", "t3"):
                return s_xlo[int(kind[1])], b + 1
            if kind in ("fc1", "fc3"):
                return s_relu[int(kind[2])], b * FC + (i + 1)
            if kind in ("y1", "y3"):
                return s_ysb[int(kind[1])], b + 1
            return s_x2, b + 1

        def last_user(n, b, offsets):
            m = n - 2
            while m >= 0 and SIDE[m][4] not in offsets:
                m -= 2
            if m >= 0:
                s, _, kind, i, off = SIDE[m]
                return freed(kind, i, b + off, s)
            s, _, kind, i, off = SIDE[m + len(SIDE)]
            return freed(kind, i, b - 1 + off, s)

        def run(eng, slot, head, tail):
            head()
            for s in range(PAIRS):
                slot(0, s, 0, (0, 1))
            with eng.Fori(1, B - 1, 2) as b:
                for ahead in range(2):
                    for s in range(PAIRS):
                        slot(b + ahead, s, (1 + ahead) % 2, (-1, 0, 1))
            for s in range(PAIRS):
                slot(B - 1, s, (B - 1) % 2, (-1, 0))
            tail()

        def side_at(s, k, offsets):
            return [(n, kind, i, off) for n, (ss, kk, kind, i, off) in enumerate(SIDE)
                    if (ss, kk) == (s, k) and off in offsets]

        block = ctx.enter_context(nc.Block())

        @block.sync
        def _(sp):
            xt = x.rearrange("b (t p) c -> b p t c", p=P)
            ot = out.rearrange("b (t p) c -> b p t c", p=P)

            def load_x(b, par):
                wait(sp, s_x1, b - 1)
                sp.dma_start(x_in[:, par, :, :], xt[b] if isinstance(b, int) else
                             xt[bass.ds(b, 1)].rearrange("b p t c -> (b p) t c")).then_inc(s_xin[par], 16)

            def store_x(b):
                wait(sp, s_x3, b + 1)
                sp.dma_start(ot[b] if isinstance(b, int) else
                             ot[bass.ds(b, 1)].rearrange("b p t c -> (b p) t c"), x3[:, :, :]).then_inc(s_stored, 16)

            load_x(0, 0)
            sp.dma_start(fc_raw.rearrange("p (t c) -> p t c", c=C), w_fc.rearrange("(t p) c -> p t c", p=P)).then_inc(s_w, 16)
            sp.dma_start(proj_raw, w_proj).then_inc(s_w, 16)
            sp.dma_start(w_raw, w_qkv).then_inc(s_w, 16)
            sp.dma_start(bias[:, :], b_out.rearrange("(a c) -> a c", a=1).to_broadcast([P, C])).then_inc(s_w, 16)
            sp.dma_start(wo[:, :, :], w_out.rearrange("(m p) c -> p m c", p=P)).then_inc(s_w, 16)
            load_x(1, 1)
            with sp.Fori(0, B // 2 - 1) as i:
                b = i * 2 + 1
                for ahead in range(2):
                    load_x(b + ahead + 1, ahead % 2)
                    store_x(b + ahead - 1)
            store_x(B - 2)
            store_x(B - 1)
            sp.wait_ge(s_stored, 16 * B)

        @block.tensor
        def _(pe):
            def product3(dst, w_hi, w_lo, m_hi, m_lo):
                pe.matmul(dst, w_hi, m_hi, start=True, stop=False)
                pe.matmul(dst, w_hi, m_lo, start=False, stop=False)
                return pe.matmul(dst, w_lo, m_hi, start=False, stop=True)

            def scores(b, p, k, par):
                i = TILES[k][0][1]
                if k == 0 or k == 1:
                    pe.wait_ge(s_glo, g_no(b, p, k))
                wait(pe, s_biased, tile_no(b, p, k - 3))
                heads = slice(TILES[k][0][0], TILES[k][-1][0] + 1)
                width = WIDTH[i]
                dst = score_bank[k % 3][:, 0:width * len(TILES[k])]
                rows = slice(i * P, (i + 1) * P)
                if len(TILES[k]) == 1:
                    hi, lo = g_hi[:, p % 2, heads.start, 0:width], g_lo[:, p % 2, heads.start, 0:width]
                else:
                    hi, lo = g_hi[:, p % 2, heads, 0:width], g_lo[:, p % 2, heads, 0:width]
                    dst = dst.rearrange("p (h n) -> p h n", h=2)
                product3(dst, xa_hi[:, par, rows], xa_lo[:, par, rows], hi, lo).then_inc(s_scores, 1)

            def turn(b, p, t):
                pe.wait_ge(s_norm, tile_no(b, p, BEATS - 1))
                n = len(TRUNS) * p + t
                bb, pp = before(b, p, 1)
                prev = turn_no(b, p, t - 2)
                wait(pe, s_turned_out, prev)
                col = 0
                for h, j in TRUNS[t]:
                    for i in range(j, NT):
                        mm = pe.transpose(turn_bank[n % 2][:, col:col + P],
                                          prob[:, p % 2, h, PCOL[i] + j * P:PCOL[i] + (j + 1) * P], ident[:, :])
                        col += P
                mm.then_inc(s_turned, 1)

            def pv(b, p, k):
                j = PVORDER[k]
                tiles = [place_of(h, j) for h in range(2)]
                pe.wait_ge(s_turned_out, turn_no(b, p, max(t for t, _ in tiles)))
                if k == 0:
                    pe.wait_ge(s_vals, v_no(b, p // 2, 1))
                    wait(pe, s_att, pair_no(b, p - 1))
                for h in range(2):
                    t, col = tiles[h]
                    width = (NT - j) * P
                    mm = pe.matmul(pv_bank[h * DH:(h + 1) * DH, j * P:N],
                                   vals[:, (p // 2) % 2, j, (p % 2) * P + h * DH:(p % 2) * P + (h + 1) * DH],
                                   probT[:, p % 2, t, col:col + width], start=(k == 0), stop=(k == 3))
                if k == 3:
                    mm.then_inc(s_pv, 1)

            def g_tile(dst, b, p, h, par):
                if (p, h) == (0, 0):
                    pe.wait_ge(s_xlo[2], b + 1)
                head = 2 * p + h
                product3(dst, a_hi[:, head, :], a_lo[:, head, :], xa_hi[:, par, :], xa_lo[:, par, :]).then_inc(s_g, 1)

            def v_tile(dst, q, i, par):
                for n in range(2):
                    rows = slice((2 * i + n) * P, (2 * i + n + 1) * P)
                    cols = slice(q * 4 * DH, (q + 1) * 4 * DH)
                    mm = product3(dst[:, n * 4 * DH:(n + 1) * 4 * DH], xa_hi[:, par, rows], xa_lo[:, par, rows],
                                  wv_hi[:, cols], wv_lo[:, cols])
                mm.then_inc(s_v, 1)

            def norm_turn(dst, w, b):
                pe.wait_ge(s_xn[w], b + 1)
                for t in range(NT):
                    mm = pe.transpose(dst[:, t * P:(t + 1) * P], xn[:, w - 1, t, :], ident[:, :])
                mm.then_inc(s_xT[w], 1)

            def fc_tile(dst, w, i, b):
                if i == 0:
                    pe.wait_ge(s_xlo[w], b + 1)
                rows = slice(i * P, (i + 1) * P)
                product3(dst, wfc_hi[:, rows], wfc_lo[:, rows], xf_hi[:, :], xf_lo[:, :]).then_inc(s_fc[w], 1)

            def y_tile(dst, w, b):
                for i in range(FC):
                    pe.wait_ge(s_hid[w], b * FC + (i + 1))
                    for t in range(NT):
                        mm = pe.matmul(dst[:, t * C:(t + 1) * C], hid[:, i, t * P:(t + 1) * P], wproj[:, i, :],
                                       start=(i == 0 and t == 0), stop=(i == FC - 1), skip_group_check=True)
                mm.then_inc(s_y[w], 1)

            def out_tile(dst, b):
                pe.wait_ge(s_att, pair_no(b, PAIRS - 1))
                for t in range(NT):
                    for m in range(PAIRS):
                        mm = pe.matmul(dst[:, t * C:(t + 1) * C], attT[:, m, t * P:(t + 1) * P], wo[:, m, :],
                                       start=(m == 0), stop=(m == PAIRS - 1))
                mm.then_inc(s_out, 1)

            def side(n, kind, i, off, b, s, par, last):
                if last:
                    wait(pe, *last)
                dst = side_bank[n % 2][:, :]
                b, par = b + off, (par + off) % 2
                if kind == "g":
                    g_tile(dst, b, (s + 1) % PAIRS, i, par)
                elif kind == "v":
                    v_tile(dst, s // 2, i, par)
                elif kind in ("t1", "t2", "t3"):
                    norm_turn(dst, int(kind[1]), b)
                elif kind in ("fc1", "fc3"):
                    fc_tile(dst, int(kind[2]), i, b)
                elif kind in ("y1", "y3"):
                    y_tile(dst, int(kind[1]), b)
                else:
                    out_tile(dst, b)

            def slot(b, s, par, offsets):
                t_of, pv_of = before(b, s, 1), before(b, s, 2)
                for k in range(BEATS):
                    if exists(b, s):
                        scores(b, s, k, par)
                    if k < 4 and exists(*pv_of):
                        pv(*pv_of, k)
                    for t in range(len(TRUNS)):
                        if TBEAT[t] == k and exists(*t_of):
                            turn(*t_of, t)
                    for n, kind, i, off in side_at(s, k, offsets):
                        side(n, kind, i, off, b, s, par, last_user(n, b, offsets))

            def chain(b, names):
                tiles = [(n, s, kind, i) for n, (s, _, kind, i, off) in enumerate(SIDE) if kind in names]
                users = {}
                for n, s, kind, i in tiles:
                    side(n, kind, i, 0, b, s, b % 2, users.get(n % 2))
                    users[n % 2] = freed(kind, i, b, s)
                return users

            def head():
                pe.wait_ge(s_const, 2)
                pe.wait_ge(s_w, 16 * 5)
                for m in range(2 * PAIRS):
                    mm = pe.transpose(banks[m // 4][:, (m % 4) * P:(m % 4 + 1) * P], w_raw[:, m * P:(m + 1) * P], ident[:, :])
                    if m % 4 == 3:
                        mm.then_inc(s_wT, 1)
                for m in range(FC):
                    mm = pe.transpose(banks[4][:, m * P:(m + 1) * P], fc_raw[:, m * P:(m + 1) * P], ident[:, :])
                mm.then_inc(s_wT, 1)
                for m in range(FC):
                    mm = pe.transpose(banks[5][:, m * P:(m + 1) * P], proj_raw[:, m * P:(m + 1) * P], ident[:, :])
                mm.then_inc(s_wT, 1)
                pe.wait_ge(s_wTcopied, 4)
                for odd in range(2):
                    for m in range(PAIRS):
                        rows = slice(odd * DH, (odd + 1) * DH)
                        mm = pe.matmul(banks[(6, 0)[odd] + m // 4][:, (m % 4) * P:(m % 4 + 1) * P],
                                       w_qkT[rows, 1, m, :], w_qkT[rows, 0, m, :], start=True, stop=True)
                        if m % 4 == 3:
                            mm.then_inc(s_a, 1)
                pe.wait_ge(s_acopied, 4)
                pe.wait_ge(s_wTcopied, 6)
                users = chain(0, ("t1", "fc1", "y1", "t2"))
                for h in range(2):
                    n = len(SIDE) - 2 + h
                    side(n, "g", h, 0, 0, PAIRS - 1, 0, users.get(n % 2))

            def tail():
                for s in range(2):
                    slot(B, s, B % 2, ())
                chain(B - 1, ("out", "t3", "fc3", "y3"))

            run(pe, slot, head, tail)

        def beat_of(kind, i):
            return [(s, k) for s, k, kk, ii, _ in SIDE if (kk, ii) == (kind, i)]

        @block.vector
        def _(dve):
            def bias_wait(b, p, k):
                dve.wait_ge(s_scores, tile_no(b, p, k))

            def bias_max(b, p, k):
                col = 0
                for h, i in TILES[k]:
                    ins = dve.tensor_tensor_reduce(negsc[:, k % 3, col:col + WIDTH[i]], score_bank[k % 3][:, col:col + WIDTH[i]],
                                                   alibi[:, 2 * p + h, N - WIDTH[i]:N], 1.0, MASKED, ALU.add, ALU.min,
                                                   negmax[:, p % 2, SEG[h, i]:SEG[h, i] + 1])
                    col += WIDTH[i]
                ins.then_inc(s_biased, 1)

            def recip(b, p, k):
                dve.wait_ge(s_exp, tile_no(b, p, k))
                cols = slice(SEG[TILES[k][0]], SEG[TILES[k][-1]] + 1)
                dve.reciprocal(rsum[:, p % 2, cols], sums[:, p % 2, cols]).then_inc(s_rsum, 1)

            def att_out(b, p):
                dve.wait_ge(s_pv, pair_no(b, p))
                if p == 0:
                    wait(dve, s_out, b)
                dve.tensor_copy(attT[:, p, :], pv_bank[:, :]).then_inc(s_att, 1)

            def stats_of(w, src, b):
                for t in range(NT):
                    ins = dve.bn_stats(stats[:, w - 1, t, :], src[:, t, :])
                ins.then_inc(s_stats[w], 1)

            def aggregate(w, b):
                for t in range(NT):
                    ins = dve.bn_aggr(meanvar[:, w - 1, t, :], stats[:, w - 1, t, :])
                ins.then_inc(s_mv[w], 1)

            def normalise(w, src, b):
                dve.wait_ge(s_rstd[w], b + 1)
                wait(dve, s_xT[w], b)
                for t in range(NT):
                    ins = dve.tensor_scalar(xn[:, w - 1, t, :], src[:, t, :], meanvar[:, w - 1, t, 0:1],
                                            rstd[:, w - 1, t:t + 1], ALU.subtract, ALU.mult)
                ins.then_inc(s_xn[w], 1)

            spike_ops = 3 * (STEPS - 1) + 1

            def spike_round(w, b, r):
                base = b * spike_ops + 3 * r
                if r == 0:
                    dve.wait_ge(s_ysb[w], b + 1)
                    dve.tensor_scalar(spikes[:, :], ysb[:, :], THRESHOLD, None, ALU.is_gt).then_inc(s_spk[w], 1)
                    dve.scalar_tensor_tensor(out=drive[:, :], in0=ysb[:, :], scalar=BETA, in1=ysb[:, :],
                                             op0=ALU.mult, op1=ALU.add).then_inc(s_spk[w], 1)
                    dve.wait_ge(s_spk[w], base + 2)
                    dve.scalar_tensor_tensor(out=negmem[:, :], in0=ysb[:, :], scalar=THRESHOLD, in1=drive[:, :],
                                             op0=ALU.is_gt, op1=ALU.subtract).then_inc(s_spk[w], 1)
                    return
                dve.wait_ge(s_spk[w], base)
                dve.scalar_tensor_tensor(out=spikes[:, :], in0=negmem[:, :], scalar=-THRESHOLD, in1=spikes[:, :],
                                         op0=ALU.is_lt, op1=ALU.add).then_inc(s_spk[w], 1)
                if r < STEPS - 1:
                    dve.scalar_tensor_tensor(out=drive[:, :], in0=negmem[:, :], scalar=-BETA, in1=ysb[:, :],
                                             op0=ALU.mult, op1=ALU.add).then_inc(s_spk[w], 1)
                    dve.wait_ge(s_spk[w], base + 2)
                    dve.scalar_tensor_tensor(out=negmem[:, :], in0=negmem[:, :], scalar=-THRESHOLD, in1=drive[:, :],
                                             op0=ALU.is_lt, op1=ALU.subtract).then_inc(s_spk[w], 1)

            def add_spikes(dst, src, w, b, done):
                dve.wait_ge(s_spk[w], b * spike_ops + spike_ops)
                dve.scalar_tensor_tensor(out=dst, in0=spikes[:, :].rearrange("p (t c) -> p t c", c=C), scalar=0.5 / STEPS,
                                         in1=src, op0=ALU.mult, op1=ALU.add).then_inc(done, 1)

            def finish1(b, par):
                add_spikes(x1[:, :, :], x_in[:, par, :, :], 1, b, s_x1)

            def stats2(b, par):
                dve.wait_ge(s_x1, b + 1)
                stats_of(2, x1, b)
                for t in range(NT):
                    ins = dve.tensor_tensor(x1b[:, par, t, :], x1[:, t, :], bias[:, :], ALU.add)
                ins.then_inc(s_x1b, 1)

            def residual2(n, b, par):
                dve.wait_ge(s_out, b + 1)
                dve.wait_ge(s_x1b, b + 1)
                dve.tensor_tensor(x2[:, :, :], side_bank[n % 2][:, :].rearrange("p (t c) -> p t c", c=C),
                                  x1b[:, par, :, :], ALU.add).then_inc(s_x2, 1)

            def stats3(b):
                dve.wait_ge(s_x2, b + 1)
                stats_of(3, x2, b)

            def finish3(b):
                wait(dve, s_stored, b * 16)
                add_spikes(x3[:, :, :], x2[:, :, :], 3, b, s_x3)

            def low_half(n, kind, i, b, s, par):
                src = side_bank[n % 2][:, :]
                if kind == "g":
                    p = (s + 1) % PAIRS
                    dve.wait_ge(s_ghi, g_no(b, p, i))
                    dve.tensor_tensor(g_lo[:, p % 2, i, :], src, g_hi[:, p % 2, i, :].bitcast(F32),
                                      ALU.subtract).then_inc(s_glo, 1)
                elif kind == "v":
                    q = s // 2
                    dve.wait_ge(s_v, v_no(b, q, i))
                    wait(dve, s_pv, pair_no(b, 2 * q - 3))
                    dve.tensor_copy(vals[:, q % 2, 2 * i:2 * i + 2, :], src.rearrange("p (t n) -> p t n", t=2)).then_inc(s_vals, 1)
                elif kind in ("t1", "t2", "t3"):
                    w = int(kind[1])
                    dve.wait_ge(s_xhi[w], b + 1)
                    hi, lo = (xa_hi[:, par, :], xa_lo[:, par, :]) if w == 2 else (xf_hi[:, :], xf_lo[:, :])
                    dve.tensor_tensor(lo, src, hi.bitcast(F32), ALU.subtract).then_inc(s_xlo[w], 1)
                elif kind == "out":
                    residual2(n, b, par)

            def steps(b, s, k, par, offsets):
                if 1 in offsets:
                    nb, npar = b + 1, 1 - par
                    if (s, k) == (0, 3):
                        dve.wait_ge(s_xin[npar], (nb - npar) * 8 + 16)
                        stats_of(1, x_in[:, npar, :, :], nb)
                    if (s, k) == (1, 1):
                        normalise(1, x_in[:, npar, :, :], nb)
                    if (s, k) in SPIKE1:
                        spike_round(1, nb, SPIKE1.index((s, k)))
                    if (s, k) == (6, 0):
                        finish1(nb, npar)
                    if (s, k) == (6, 1):
                        stats2(nb, npar)
                    if (s, k) == (7, 1):
                        normalise(2, x1, nb)
                if -1 in offsets:
                    if (s, k) == (2, 2):
                        stats3(b - 1)
                    if (s, k) == (3, 0):
                        normalise(3, x2, b - 1)
                    if (s, k) in SPIKE3:
                        spike_round(3, b - 1, SPIKE3.index((s, k)))
                    if (s, k) == (7, 5):
                        finish3(b - 1)

            AGGREGATE = [((0, 5), 1, 1), ((2, 4), 3, -1), ((6, 3), 2, 1)]
            SPIKE1 = [(4, 4), (5, 0), (5, 2), (5, 4), (5, 5)]
            SPIKE3 = [(6, 5), (7, 0), (7, 2), (7, 3), (7, 4)]

            def slot(b, s, par, offsets):
                for k in range(BEATS):
                    for at, w, off in AGGREGATE:
                        if at == (s, k) and off in offsets:
                            dve.wait_ge(s_stats[w], b + off + 1)
                    if exists(b, s):
                        bias_wait(b, s, k)
                    last = (b, s, k - 2) if k >= 2 else (*before(b, s, 1), BEATS + k - 2)
                    if exists(*last[:2]):
                        recip(*last)
                    if exists(b, s):
                        bias_max(b, s, k)
                    for at, w, off in AGGREGATE:
                        if at == (s, k) and off in offsets:
                            aggregate(w, b + off)
                    if k == 4 and exists(*before(b, s, 2)):
                        att_out(*before(b, s, 2))
                    for n, kind, i, off in side_at(s, k - 1, offsets):
                        low_half(n, kind, i, b + off, s, (par + off) % 2)
                    steps(b, s, k, par, offsets)

            def number(kind):
                return [n for n, x in enumerate(SIDE) if x[2] == kind][0]

            def head():
                qkT = w_qkT.rearrange("p t m c -> p (t m c)")
                for m in range(4):
                    dve.wait_ge(s_wT, m + 1)
                    dve.tensor_copy(qkT[:, m * 512:(m + 1) * 512], banks[m][:, :]).then_inc(s_wTcopied, 1)
                dve.wait_ge(s_wT, 5)
                dve.tensor_copy(wfc_hi[:, :], banks[4][:, :]).then_inc(s_split, 1)
                dve.wait_ge(s_split, 1)
                dve.tensor_tensor(wfc_lo[:, :], banks[4][:, :], wfc_hi[:, :].bitcast(F32), ALU.subtract).then_inc(s_wTcopied, 1)
                dve.wait_ge(s_wT, 6)
                dve.tensor_copy(wproj[:, :, :].rearrange("p t c -> p (t c)"), banks[5][:, :]).then_inc(s_wTcopied, 1)
                for odd in range(2):
                    for half in range(2):
                        n = 2 * odd + half
                        dve.wait_ge(s_a, n + 1)
                        src = banks[(6, 0)[odd] + half][:, :].rearrange("p (m c) -> p m c", c=C)
                        heads = slice(8 * half + odd, 8 * half + odd + 7, 2)
                        dve.tensor_scalar(a_hi[:, heads, :], src, -SCALE, None, ALU.mult).then_inc(s_split, 1)
                        dve.wait_ge(s_split, n + 2)
                        dve.scalar_tensor_tensor(out=a_lo[:, heads, :], in0=src, scalar=-SCALE,
                                                 in1=a_hi[:, heads, :].bitcast(F32), op0=ALU.mult,
                                                 op1=ALU.subtract).then_inc(s_acopied, 1)
                dve.tensor_copy(wv_hi[:, :], w_raw[:, 2 * INNER:3 * INNER]).then_inc(s_split, 1)
                dve.wait_ge(s_split, 6)
                dve.tensor_tensor(wv_lo[:, :], w_raw[:, 2 * INNER:3 * INNER], wv_hi[:, :].bitcast(F32),
                                  ALU.subtract).then_inc(s_split, 1)
                dve.wait_ge(s_split, 7)
                dve.wait_ge(s_xin[0], 16)
                stats_of(1, x_in[:, 0, :, :], 0)
                dve.wait_ge(s_stats[1], 1)
                aggregate(1, 0)
                dve.wait_ge(s_const, 3)
                for h in range(HEADS):
                    ins = dve.tensor_scalar(alibi[:, h, :], dist[:, :], SLOPES[h], None, ALU.mult)
                ins.then_inc(s_alibi, 1)
                normalise(1, x_in[:, 0, :, :], 0)
                low_half(number("t1"), "t1", 0, 0, 0, 0)
                for r in range(STEPS):
                    spike_round(1, 0, r)
                finish1(0, 0)
                stats2(0, 0)
                dve.wait_ge(s_stats[2], 1)
                aggregate(2, 0)
                normalise(2, x1, 0)
                low_half(number("t2"), "t2", 0, 0, 0, 0)
                for h in range(2):
                    low_half(len(SIDE) - 2 + h, "g", h, 0, PAIRS - 1, 0)
                dve.wait_ge(s_alibi, 1)

            def tail():
                for s in range(2):
                    slot(B, s, B % 2, ())
                b = B - 1
                low_half(number("out"), "out", 0, b, 0, b % 2)
                stats3(b)
                dve.wait_ge(s_stats[3], b + 1)
                aggregate(3, b)
                normalise(3, x2, b)
                low_half(number("t3"), "t3", 0, b, 0, b % 2)
                for r in range(STEPS):
                    spike_round(3, b, r)
                finish3(b)

            run(dve, slot, head, tail)

        @block.scalar
        def _(act):
            def exps(b, p, k):
                act.wait_ge(s_biased, tile_no(b, p, k))
                if k == 0:
                    bb, pp = before(b, p, 2)
                    wait(act, s_turned, turn_no(bb, pp, len(TRUNS) - 1))
                col = 0
                for h, i in TILES[k]:
                    seg = SEG[h, i]
                    ins = act.activation(prob[:, p % 2, h, PCOL[i]:PCOL[i] + WIDTH[i]], negsc[:, k % 3, col:col + WIDTH[i]],
                                         ACT.Exp, bias=negmax[:, p % 2, seg:seg + 1], scale=-1.0,
                                         accum_out=sums[:, p % 2, seg:seg + 1])
                    col += WIDTH[i]
                ins.then_inc(s_exp, 1)

            def turned_out(b, p, t):
                act.wait_ge(s_turned, turn_no(b, p, t))
                if t == 0:
                    bb, pp = before(b, p, 2)
                    wait(act, s_pv, pair_no(bb, pp))
                act.copy(probT[:, p % 2, t, :], turn_bank[(len(TRUNS) * p + t) % 2][:, :]).then_inc(s_turned_out, 1)

            def high_half(n, kind, i, b, s, par):
                src = side_bank[n % 2][:, :]
                if kind == "g":
                    p = (s + 1) % PAIRS
                    act.wait_ge(s_g, g_no(b, p, i))
                    act.copy(g_hi[:, p % 2, i, :], src).then_inc(s_ghi, 1)
                elif kind in ("t1", "t2", "t3"):
                    w = int(kind[1])
                    act.wait_ge(s_xT[w], b + 1)
                    hi = xa_hi[:, par, :] if w == 2 else xf_hi[:, :]
                    if w == 1:
                        wait(act, s_fc[3], (b - 2) * FC)
                    if w == 3:
                        wait(act, s_fc[1], (b + 2) * FC + FC if not isinstance(b, int) else (min(b + 2, B - 1) + 1) * FC)
                    act.copy(hi, src).then_inc(s_xhi[w], 1)
                elif kind in ("fc1", "fc3"):
                    w = int(kind[2])
                    act.wait_ge(s_fc[w], b * FC + (i + 1))
                    if i >= 2:
                        act.wait_ge(s_hid[w], b * FC + (i - 1))
                    act.activation(relu[:, i % 2, :], src, ACT.Relu).then_inc(s_relu[w], 1)
                elif kind in ("y1", "y3"):
                    w = int(kind[1])
                    act.wait_ge(s_y[w], b + 1)
                    if w == 1:
                        wait(act, s_x3, b - 2)
                    else:
                        wait(act, s_x1, b + 3 if not isinstance(b, int) else min(b + 3, B))
                    act.copy(ysb[:, :], src).then_inc(s_ysb[w], 1)

            def slot(b, s, par, offsets):
                for k in range(BEATS):
                    for n, kind, i, off in side_at(s, k - 1, offsets):
                        high_half(n, kind, i, b + off, s, (par + off) % 2)
                    if exists(b, s):
                        exps(b, s, k)
                    for t in range(len(TRUNS)):
                        if TBEAT[t] == k and exists(*before(b, s, 1)):
                            turned_out(*before(b, s, 1), t)

            def chain(b, names):
                for n, (s, _, kind, i, off) in enumerate(SIDE):
                    if kind in names:
                        high_half(n, kind, i, b, s, b % 2)

            def head():
                chain(0, ("t1", "fc1", "y1", "t2"))
                for h in range(2):
                    high_half(len(SIDE) - 2 + h, "g", h, 0, PAIRS - 1, 0)

            def tail():
                for s in range(2):
                    slot(B, s, B % 2, ())
                chain(B - 1, ("t3", "fc3", "y3"))

            run(act, slot, head, tail)

        @block.gpsimd
        def _(pool):
            def norm(b, p, k):
                pool.wait_ge(s_rsum, tile_no(b, p, k))
                for h, i in TILES[k]:
                    seg = SEG[h, i]
                    pr = prob[:, p % 2, h, PCOL[i]:PCOL[i] + WIDTH[i]]
                    ins = pool.tensor_tensor(pr, pr, rsum[:, p % 2, seg:seg + 1].to_broadcast([P, WIDTH[i]]), ALU.mult)
                ins.then_inc(s_norm, 1)

            def square(w, i, b, offsets=(1,)):
                pool.wait_ge(s_relu[w], b * FC + (i + 1))
                if i == 0:
                    if w == 1:
                        wait(pool, s_y[3], b - 2)
                    else:
                        wait(pool, s_y[1], b + 3 if not isinstance(b, int) else min(b + 3, B))
                pool.tensor_tensor(hid[:, i, :], relu[:, i % 2, :], relu[:, i % 2, :], ALU.mult).then_inc(s_hid[w], 1)

            def inverse_std(w, b):
                pool.wait_ge(s_mv[w], b + 1)
                pool.tensor_tensor(vareps[:, w - 1, :], meanvar[:, w - 1, :, 1], eps[:, :], ALU.add).then_inc(s_ve[w], 1)
                pool.wait_ge(s_ve[w], b + 1)
                pool.tensor_tensor(rstd[:, w - 1, :], vareps[:, w - 1, :], minus_half[:, :], ALU.pow).then_inc(s_rstd[w], 1)

            def slot(b, s, par, offsets):
                for k in range(BEATS):
                    last = (b, s, k - 2) if k >= 2 else (*before(b, s, 1), BEATS + k - 2)
                    if exists(*last[:2]):
                        norm(*last)
                    for n, kind, i, off in side_at(s, k - 1, offsets):
                        if kind in ("fc1", "fc3"):
                            square(int(kind[2]), i, b + off)
                    for at, w, off in (((0, 5), 1, 1), ((2, 5), 3, -1), ((6, 4), 2, 1)):
                        if at == (s, k) and off in offsets:
                            inverse_std(w, b + off)

            def head():
                pool.memset(ident[:, :], 0.0).then_inc(s_const0, 1)
                pool.iota(dist[:, :], pattern=[[-1, N]], base=N - P, channel_multiplier=1,
                          allow_small_or_imprecise_dtypes=True).then_inc(s_dist0, 1)
                pool.memset(eps[:, :], EPS)
                pool.memset(minus_half[:, :], -0.5).then_inc(s_const, 1)
                pool.wait_ge(s_const0, 1)
                pool.affine_select(out=ident[:, :], in_=ident[:, :], compare_op=ALU.not_equal, fill=1.0, base=0,
                                   pattern=[[-1, P]], channel_multiplier=1).then_inc(s_const, 1)
                pool.wait_ge(s_dist0, 1)
                pool.affine_select(out=dist[:, :], in_=dist[:, :], compare_op=ALU.is_ge, fill=MASKED, base=N - P,
                                   pattern=[[-1, N]], channel_multiplier=1).then_inc(s_const, 1)
                pool.wait_ge(s_const, 1)
                inverse_std(1, 0)
                for i in range(FC):
                    square(1, i, 0)
                inverse_std(2, 0)

            def tail():
                for s in range(2):
                    slot(B, s, B % 2, ())
                inverse_std(3, B - 1)
                for i in range(FC):
                    square(3, i, B - 1)

            run(pool, slot, head, tail)


_INS = ['L0_attn_x', 'L0_attn_w_qkv', 'L0_attn_w_out', 'L0_attn_b_out', 'L0_ffn_W_fc', 'L0_ffn_W_proj']
_OUTS = [((16, 512, 128), 'float32')]


def kernel(**inputs):
    import numpy as _np
    import concourse.bacc as _bacc
    from concourse import mybir as _mybir
    from concourse.bass_utils import run_bass_kernel_spmd as _run

    nc = _bacc.Bacc("TRN2", target_bir_lowering=False, num_devices=1)
    arrays, args = {}, []
    for name in _INS:
        a = _np.ascontiguousarray(inputs[name])
        arrays[f"in_{name}_dram"] = a
        args.append(nc.dram_tensor(f"in_{name}_dram", a.shape, _mybir.dt.from_np(a.dtype), kind="ExternalInput").ap())
    for i, (shape, dtype) in enumerate(_OUTS):
        dt = _mybir.dt.from_np(_np.dtype(dtype))
        args.append(nc.dram_tensor(f"out_{i}_dram", shape, dt, kind="ExternalOutput").ap())
    macaron_kernel(nc, *args)
    r = _run(nc, [arrays], core_ids=[0])
    got = tuple(r.results[0][f"out_{i}_dram"] for i in range(len(_OUTS)))
    return got[0]
```

```python
from contextlib import ExitStack

import concourse.bass as bass
from concourse import mybir

ALU = mybir.AluOpType
ACT = mybir.ActivationFunctionType
F32 = mybir.dt.float32
F32R = mybir.dt.float32r

P = 128
B, N, C = 16, 512, 128
HEADS, DH = 16, 64
F = 4 * C
NT = N // P
FC = F // P
PAIRS = HEADS // 2
INNER = HEADS * DH
SCALE = DH ** -0.5
EPS = 1e-5
BETA, THRESHOLD, STEPS = 0.9, 1.0, 5
SLOPES = [2.0 ** (-0.5 * (h + 1)) for h in range(HEADS)]
MASKED = 3.0e38

TILES = [[(0, 3)], [(0, 2)], [(1, 3)], [(1, 2)], [(0, 1), (1, 1)], [(0, 0), (1, 0)]]
BEATS = len(TILES)
SEG = {hi: n for n, hi in enumerate(x for t in TILES for x in t)}
SEG_TILE = {hi: k for k, t in enumerate(TILES) for hi in t}
WIDTH = [(i + 1) * P for i in range(NT)]
PCOL = [sum(WIDTH[i + 1:]) for i in range(NT)]
PHEAD = sum(WIDTH)
TRUNS = [[(0, 2), (1, 2)], [(0, 1), (0, 3)], [(1, 1), (1, 3)], [(0, 0)], [(1, 0)]]
TNEEDS = [max(SEG_TILE[h, i] for h, j in runs for i in range(j, NT)) for runs in TRUNS]
TBEAT = [1, 2, 3, 4, 5]
ATTBEAT = 5
PV = [[], [2], [1], [3], [0], []]
PVORDER = [j for js in PV for j in js]
GBEAT_LAST = [3, 4]
GBEAT = [3, 4]


def place_of(h, j):
    for t, runs in enumerate(TRUNS):
        col = 0
        for hh, jj in runs:
            if (hh, jj) == (h, j):
                return t, col
            col += (NT - jj) * P


def beats_from(slot, beat, counts):
    at = [divmod(slot * BEATS + beat + n, BEATS) for n in range(len(counts))]
    return [x for x, c in zip(at, counts) for _ in range(c)]


SIDE = sorted(
    [(s, (GBEAT if s < PAIRS - 1 else GBEAT_LAST)[h], "g", h, 0 if s < PAIRS - 1 else 1) for s in range(PAIRS) for h in range(2)]
    + [(s, i, "v", i, 0) for s in range(1, PAIRS, 2) for i in range(2)]
    + [(0, 4, "t1", 0, 1), (1, 2, "fc1", 0, 1), (1, 3, "fc1", 1, 1), (1, 4, "fc1", 2, 1), (2, 0, "fc1", 3, 1),
       (2, 3, "y1", 0, 1), (2, 4, "y1", 1, 1), (6, 1, "t2", 0, 1)]
    + [(2, 1, "out", 0, -1), (2, 2, "out", 1, -1), (2, 5, "out", 2, -1), (3, 2, "out", 3, -1),
       (4, 3, "t3", 0, -1), (5, 2, "fc3", 0, -1), (5, 3, "fc3", 1, -1), (5, 4, "fc3", 2, -1), (6, 0, "fc3", 3, -1),
       (6, 2, "y3", 0, -1), (6, 3, "y3", 1, -1)],
    key=lambda x: (x[0], x[1], x[2] == "g"))
SPIKE1 = beats_from(3, 0, [1] * 14)
SPIKE3 = beats_from(6, 4, [1, 1, 2, 2, 2, 2, 2, 2])
LN1 = dict(stats=(0, 0), aggregate=(0, 1), rstd=(0, 1), normalise=(0, 3))
LN2 = dict(stats=(5, 2), aggregate=(5, 3), rstd=(5, 4), normalise=(6, 0))
LN3 = dict(stats=(3, 4), aggregate=(3, 5), rstd=(4, 0), normalise=(4, 1))


def macaron_kernel(nc: bass.Bass, x, w_qkv, w_out, b_out, w_fc, w_proj, out):
    ctx = ExitStack()
    with ctx:
        def sb(name, shape, dt=F32):
            return ctx.enter_context(nc.sbuf_tensor(name, shape, dt))

        def sem(name):
            return ctx.enter_context(nc.semaphore(name))

        banks = [ctx.enter_context(nc.psum_tensor(f"bank{i}", [P, 512], F32)) for i in range(8)]
        score_bank, turn_bank, pv_bank, side_bank = banks[0:3], banks[3:5], banks[5], banks[6:8]

        ident = sb("ident", [P, P])
        minus_half = sb("minus_half", [P, NT])
        eps = sb("eps", [P, NT])
        alibi = sb("alibi", [P, HEADS, N])
        a_hi = sb("a_hi", [P, HEADS, C], F32R)
        a_lo = sb("a_lo", [P, HEADS, C], F32R)
        wv_hi = sb("wv_hi", [P, INNER], F32R)
        wv_lo = sb("wv_lo", [P, INNER], F32R)
        wo = sb("wo", [P, PAIRS, C])
        wfc_hi = sb("wfc_hi", [P, F], F32R)
        wfc_lo = sb("wfc_lo", [P, F], F32R)
        wproj = sb("wproj", [P, FC, C])
        bias = sb("bias", [P, C])
        x_in = sb("x_in", [P, 2, NT, C])
        x1b = sb("x1b", [P, 2, NT, C])
        x1 = sb("x1", [P, NT, C])
        x2 = sb("x2", [P, NT, C])
        x3 = sb("x3", [P, NT, C])
        xn = sb("xn", [P, 2, NT, C])
        stats = sb("stats", [P, 3, NT, 6])
        meanvar = sb("meanvar", [P, 3, NT, 2])
        vareps = sb("vareps", [P, 3, NT])
        rstd = sb("rstd", [P, 3, NT])
        xf_hi = sb("xf_hi", [P, N], F32R)
        xf_lo = sb("xf_lo", [P, N], F32R)
        xa_hi = sb("xa_hi", [P, 2, N], F32R)
        xa_lo = sb("xa_lo", [P, 2, N], F32R)
        relu = sb("relu", [P, 2, N])
        hid = sb("hid", [P, FC, N])
        ysb = sb("ysb", [P, N])
        negmem = sb("negmem", [P, N])
        drive = sb("drive", [P, N])
        spikes = sb("spikes", [P, N])
        g_hi = sb("g_hi", [P, 2, 2, N], F32R)
        g_lo = sb("g_lo", [P, 2, 2, N], F32R)
        vals = sb("vals", [P, 2, NT, 4 * DH])
        negsc = sb("negsc", [P, 3, N])
        negmax = sb("negmax", [P, 2, 8])
        sums = sb("sums", [P, 2, 8])
        rsum = sb("rsum", [P, 2, 8])
        prob = sb("prob", [P, 2, 2, PHEAD])
        probT = sb("probT", [P, 2, len(TRUNS), N])
        attT = sb("attT", [P, PAIRS + 2, N])
        w_raw = prob[:, :, :, :].rearrange("p a h n -> p (a h n)")[:, 0:3 * INNER]
        w_qkT = prob[:, :, :, :].rearrange("p a h n -> p (a h n)")[:, 3 * INNER:5 * INNER].rearrange(
            "p (t m c) -> p t m c", t=2, c=C)
        dist = probT[:, 1, 0, :]
        fc_raw, proj_raw = probT[:, 0, 0, :], probT[:, 0, 1, :]

        s_w, s_stored = sem("s_w"), sem("s_stored")
        s_xin = [sem("s_xin_even"), sem("s_xin_odd")]
        s_const, s_const0, s_dist0, s_wT, s_wTcopied = sem("s_const"), sem("s_const0"), sem("s_dist0"), sem("s_wT"), sem("s_wTcopied")
        s_a, s_acopied, s_split, s_alibi = sem("s_a"), sem("s_acopied"), sem("s_split"), sem("s_alibi")
        s_scores, s_biased, s_exp, s_rsum, s_norm = (sem(n) for n in ("s_scores", "s_biased", "s_exp", "s_rsum", "s_norm"))
        s_turned, s_turned_out, s_pv, s_att = (sem(n) for n in ("s_turned", "s_turned_out", "s_pv", "s_att"))
        s_g, s_ghi, s_glo, s_v, s_vals = (sem(n) for n in ("s_g", "s_ghi", "s_glo", "s_v", "s_vals"))
        s_fc, s_relu, s_hid, s_y, s_ysb, s_spk = (
            {w: sem(f"{n}{w}") for w in (1, 3)} for n in ("s_fc", "s_relu", "s_hid", "s_y", "s_ysb", "s_spk"))
        s_stats, s_mv, s_ve, s_rstd, s_xn, s_xT, s_xhi, s_xlo = (
            {w: sem(f"{n}{w}") for w in (1, 2, 3)}
            for n in ("s_stats", "s_mv", "s_ve", "s_rstd", "s_xn", "s_xT", "s_xhi", "s_xlo"))
        s_out, s_x1, s_x1b, s_x2, s_x3 = (sem(n) for n in ("s_out", "s_x1", "s_x1b", "s_x2", "s_x3"))

        def wait(eng, semaphore, value):
            if not isinstance(value, int) or value > 0:
                eng.wait_ge(semaphore, value)

        def tile_no(b, p, k):
            return b * (PAIRS * BEATS) + (p * BEATS + k + 1)

        def turn_no(b, p, t):
            return b * (PAIRS * len(TRUNS)) + (p * len(TRUNS) + t + 1)

        def pair_no(b, p):
            return b * PAIRS + (p + 1)

        def g_no(b, p, h):
            return b * HEADS + (2 * p + h + 1)

        def v_no(b, q, i):
            return b * PAIRS + (2 * q + i + 1)

        def before(b, p, back):
            return (b, p - back) if p >= back else (b - 1, p - back + PAIRS)

        def exists(b, p):
            return not isinstance(b, int) or (0 <= b < B)

        def freed(kind, i, b, s):
            if kind == "g":
                return s_glo, g_no(b, (s + 1) % PAIRS, i)
            if kind == "v":
                return s_vals, v_no(b, s // 2, i)
            if kind in ("t1", "t2", "t3"):
                return s_xlo[int(kind[1])], b + 1
            if kind in ("fc1", "fc3"):
                return s_relu[int(kind[2])], b * FC + (i + 1)
            if kind in ("y1", "y3"):
                return s_ysb[int(kind[1])], b * 2 + (i + 1)
            return s_x2, b * NT + (i + 1)

        def last_user(n, b, offsets):
            for m in range(n - 1, -1, -1):
                s, _, kind, i, off = SIDE[m]
                if m % 2 == n % 2 and off in offsets:
                    return freed(kind, i, b + off, s)
            m = len(SIDE) - 1 - (len(SIDE) - 1 - n) % 2
            s, _, kind, i, off = SIDE[m]
            assert kind == "g"
            return freed(kind, i, b - 1 + off, s)

        def att_at(p, par):
            return PAIRS + p if p < 2 and par else p

        def run(eng, slot, head, tail):
            head()
            for s in range(PAIRS):
                slot(0, s, 0, (0, 1))
            with eng.Fori(1, B - 1, 2) as b:
                for ahead in range(2):
                    for s in range(PAIRS):
                        slot(b + ahead, s, (1 + ahead) % 2, (-1, 0, 1))
            for s in range(PAIRS):
                slot(B - 1, s, (B - 1) % 2, (-1, 0))
            tail()

        def side_at(s, k, offsets):
            s, k = (s, k) if k >= 0 else (s - 1, BEATS - 1)
            return [(n, kind, i, off, s) for n, (ss, kk, kind, i, off) in enumerate(SIDE)
                    if (ss, kk) == (s, k) and off in offsets]

        block = ctx.enter_context(nc.Block())

        @block.sync
        def _(sp):
            xt = x.rearrange("b (t p) c -> b p t c", p=P)
            ot = out.rearrange("b (t p) c -> b p t c", p=P)

            def load_x(b, par):
                wait(sp, s_x1, b - 1)
                sp.dma_start(x_in[:, par, :, :], xt[b] if isinstance(b, int) else
                             xt[bass.ds(b, 1)].rearrange("b p t c -> (b p) t c")).then_inc(s_xin[par], 16)

            def store_x(b):
                wait(sp, s_x3, b + 1)
                sp.dma_start(ot[b] if isinstance(b, int) else
                             ot[bass.ds(b, 1)].rearrange("b p t c -> (b p) t c"), x3[:, :, :]).then_inc(s_stored, 16)

            load_x(0, 0)
            sp.dma_start(fc_raw.rearrange("p (t c) -> p t c", c=C), w_fc.rearrange("(t p) c -> p t c", p=P)).then_inc(s_w, 16)
            sp.dma_start(proj_raw, w_proj).then_inc(s_w, 16)
            sp.dma_start(w_raw, w_qkv).then_inc(s_w, 16)
            sp.dma_start(bias[:, :], b_out.rearrange("(a c) -> a c", a=1).to_broadcast([P, C])).then_inc(s_w, 16)
            sp.dma_start(wo[:, :, :], w_out.rearrange("(m p) c -> p m c", p=P)).then_inc(s_w, 16)
            load_x(1, 1)
            load_x(2, 0)
            with sp.Fori(0, B // 2 - 2) as i:
                for ahead in range(2):
                    load_x(i * 2 + 3 + ahead, 1 - ahead)
                    store_x(i * 2 + ahead)
            load_x(B - 1, 1)
            for b in range(B - 4, B):
                store_x(b)
            sp.wait_ge(s_stored, 16 * B)

        @block.tensor
        def _(pe):
            def product3(dst, w_hi, w_lo, m_hi, m_lo):
                pe.matmul(dst, w_hi, m_hi, start=True, stop=False)
                pe.matmul(dst, w_hi, m_lo, start=False, stop=False)
                return pe.matmul(dst, w_lo, m_hi, start=False, stop=True)

            def scores(b, p, k, par):
                i = TILES[k][0][1]
                if i == NT - 1:
                    pe.wait_ge(s_glo, g_no(b, p, TILES[k][0][0]))
                wait(pe, s_biased, tile_no(b, p, k - 3))
                heads = slice(TILES[k][0][0], TILES[k][-1][0] + 1)
                width = WIDTH[i]
                dst = score_bank[k % 3][:, 0:width * len(TILES[k])]
                rows = slice(i * P, (i + 1) * P)
                if len(TILES[k]) == 1:
                    hi, lo = g_hi[:, p % 2, heads.start, 0:width], g_lo[:, p % 2, heads.start, 0:width]
                else:
                    hi, lo = g_hi[:, p % 2, heads, 0:width], g_lo[:, p % 2, heads, 0:width]
                    dst = dst.rearrange("p (h n) -> p h n", h=2)
                product3(dst, xa_hi[:, par, rows], xa_lo[:, par, rows], hi, lo).then_inc(s_scores, 1)

            def turn(b, p, t):
                pe.wait_ge(s_norm, tile_no(b, p, TNEEDS[t]))
                n = len(TRUNS) * p + t
                bb, pp = before(b, p, 1)
                prev = turn_no(b, p, t - 2)
                wait(pe, s_turned_out, prev)
                col = 0
                for h, j in TRUNS[t]:
                    for i in range(j, NT):
                        mm = pe.transpose(turn_bank[n % 2][:, col:col + P],
                                          prob[:, p % 2, h, PCOL[i] + j * P:PCOL[i] + (j + 1) * P], ident[:, :])
                        col += P
                mm.then_inc(s_turned, 1)

            def pv(b, p, j):
                tiles = [place_of(h, j) for h in range(2)]
                pe.wait_ge(s_turned_out, turn_no(b, p, max(t for t, _ in tiles)))
                if j == PVORDER[0]:
                    pe.wait_ge(s_vals, v_no(b, p // 2, 1))
                    wait(pe, s_att, pair_no(b, p - 1))
                for h in range(2):
                    t, col = tiles[h]
                    width = (NT - j) * P
                    mm = pe.matmul(pv_bank[h * DH:(h + 1) * DH, j * P:N],
                                   vals[:, (p // 2) % 2, j, (p % 2) * P + h * DH:(p % 2) * P + (h + 1) * DH],
                                   probT[:, p % 2, t, col:col + width], start=(j == PVORDER[0]),
                                   stop=(j == PVORDER[-1]), skip_group_check=True)
                if j == PVORDER[-1]:
                    mm.then_inc(s_pv, 1)

            def g_tile(dst, b, p, h, par):
                if (p, h) == (0, 0):
                    pe.wait_ge(s_xlo[2], b + 1)
                head = 2 * p + h
                product3(dst, a_hi[:, head, :], a_lo[:, head, :], xa_hi[:, par, :], xa_lo[:, par, :]).then_inc(s_g, 1)

            def v_tile(dst, q, i, par):
                for n in range(2):
                    rows = slice((2 * i + n) * P, (2 * i + n + 1) * P)
                    cols = slice(q * 4 * DH, (q + 1) * 4 * DH)
                    mm = product3(dst[:, n * 4 * DH:(n + 1) * 4 * DH], xa_hi[:, par, rows], xa_lo[:, par, rows],
                                  wv_hi[:, cols], wv_lo[:, cols])
                mm.then_inc(s_v, 1)

            def norm_turn(dst, w, b):
                pe.wait_ge(s_xn[w], b + 1)
                for t in range(NT):
                    mm = pe.transpose(dst[:, t * P:(t + 1) * P], xn[:, w % 2, t, :], ident[:, :])
                mm.then_inc(s_xT[w], 1)

            def fc_tile(dst, w, i, b):
                if i == 0:
                    pe.wait_ge(s_xlo[w], b + 1)
                rows = slice(i * P, (i + 1) * P)
                product3(dst, wfc_hi[:, rows], wfc_lo[:, rows], xf_hi[:, :], xf_lo[:, :]).then_inc(s_fc[w], 1)

            def y_tile(dst, w, half, b):
                for i in range(FC):
                    pe.wait_ge(s_hid[w], b * FC + (i + 1))
                    for t in range(2):
                        rows = slice((2 * half + t) * P, (2 * half + t + 1) * P)
                        mm = pe.matmul(dst[:, t * C:(t + 1) * C], hid[:, i, rows], wproj[:, i, :],
                                       start=(i == 0 and t == 0), stop=(i == FC - 1), skip_group_check=True)
                mm.then_inc(s_y[w], 1)

            def out_tile(dst, t, b, par):
                pe.wait_ge(s_att, pair_no(b, PAIRS - 1))
                for m in range(PAIRS):
                    mm = pe.matmul(dst[:, 0:C], attT[:, att_at(m, par), t * P:(t + 1) * P], wo[:, m, :],
                                   start=(m == 0), stop=(m == PAIRS - 1))
                mm.then_inc(s_out, 1)

            def side(n, kind, i, off, b, s, par, last):
                if last:
                    wait(pe, *last)
                dst = side_bank[n % 2][:, :]
                b, par = b + off, (par + off) % 2
                if kind == "g":
                    g_tile(dst, b, (s + 1) % PAIRS, i, par)
                elif kind == "v":
                    v_tile(dst, s // 2, i, par)
                elif kind in ("t1", "t2", "t3"):
                    norm_turn(dst, int(kind[1]), b)
                elif kind in ("fc1", "fc3"):
                    fc_tile(dst, int(kind[2]), i, b)
                elif kind in ("y1", "y3"):
                    y_tile(dst, int(kind[1]), i, b)
                else:
                    out_tile(dst, i, b, par)

            def slot(b, s, par, offsets):
                t_of, pv_of = before(b, s, 1), before(b, s, 2)
                for k in range(BEATS):
                    if exists(b, s):
                        scores(b, s, k, par)
                    for j in PV[k]:
                        if exists(*pv_of):
                            pv(*pv_of, j)
                    for t in range(len(TRUNS)):
                        if TBEAT[t] == k and exists(*t_of):
                            turn(*t_of, t)
                    for n, kind, i, off, _ in side_at(s, k, offsets):
                        side(n, kind, i, off, b, s, par, last_user(n, b, offsets))

            def chain(b, names):
                tiles = [(n, s, kind, i) for n, (s, _, kind, i, off) in enumerate(SIDE) if kind in names]
                users = {}
                for n, s, kind, i in tiles:
                    side(n, kind, i, 0, b, s, b % 2, users.get(n % 2))
                    users[n % 2] = freed(kind, i, b, s)
                return users

            def head():
                pe.wait_ge(s_const, 2)
                pe.wait_ge(s_w, 16 * 5)
                for m in range(2 * PAIRS):
                    mm = pe.transpose(banks[m // 4][:, (m % 4) * P:(m % 4 + 1) * P], w_raw[:, m * P:(m + 1) * P], ident[:, :])
                    if m % 4 == 3:
                        mm.then_inc(s_wT, 1)
                for m in range(FC):
                    mm = pe.transpose(banks[4][:, m * P:(m + 1) * P], fc_raw[:, m * P:(m + 1) * P], ident[:, :])
                mm.then_inc(s_wT, 1)
                for m in range(FC):
                    mm = pe.transpose(banks[5][:, m * P:(m + 1) * P], proj_raw[:, m * P:(m + 1) * P], ident[:, :])
                mm.then_inc(s_wT, 1)
                pe.wait_ge(s_wTcopied, 4)
                for odd in range(2):
                    for m in range(PAIRS):
                        rows = slice(odd * DH, (odd + 1) * DH)
                        mm = pe.matmul(banks[(6, 0)[odd] + m // 4][:, (m % 4) * P:(m % 4 + 1) * P],
                                       w_qkT[rows, 1, m, :], w_qkT[rows, 0, m, :], start=True, stop=True)
                        if m % 4 == 3:
                            mm.then_inc(s_a, 1)
                pe.wait_ge(s_acopied, 4)
                pe.wait_ge(s_wTcopied, 6)
                users = chain(0, ("t1", "fc1", "y1", "t2"))
                for h in range(2):
                    n = len(SIDE) - 2 + h
                    side(n, "g", h, 0, 0, PAIRS - 1, 0, users.get(n % 2))

            def tail():
                for s in range(2):
                    slot(B, s, B % 2, ())
                chain(B - 1, ("out", "t3", "fc3", "y3"))

            run(pe, slot, head, tail)

        @block.vector
        def _(dve):
            def bias_wait(b, p, k):
                dve.wait_ge(s_scores, tile_no(b, p, k))

            def bias_max(b, p, k):
                col = 0
                for h, i in TILES[k]:
                    ins = dve.tensor_tensor_reduce(negsc[:, k % 3, col:col + WIDTH[i]], score_bank[k % 3][:, col:col + WIDTH[i]],
                                                   alibi[:, 2 * p + h, N - WIDTH[i]:N], 1.0, MASKED, ALU.add, ALU.min,
                                                   negmax[:, p % 2, SEG[h, i]:SEG[h, i] + 1])
                    col += WIDTH[i]
                ins.then_inc(s_biased, 1)

            def recip(b, p, k):
                dve.wait_ge(s_exp, tile_no(b, p, k))
                cols = slice(SEG[TILES[k][0]], SEG[TILES[k][-1]] + 1)
                dve.reciprocal(rsum[:, p % 2, cols], sums[:, p % 2, cols]).then_inc(s_rsum, 1)

            def stats_of(w, src, b):
                for t in range(NT):
                    ins = dve.bn_stats(stats[:, w - 1, t, :], src[:, t, :])
                ins.then_inc(s_stats[w], 1)

            def aggregate(w, b):
                for t in range(NT):
                    ins = dve.bn_aggr(meanvar[:, w - 1, t, :], stats[:, w - 1, t, :])
                ins.then_inc(s_mv[w], 1)

            def normalise(w, src, b):
                dve.wait_ge(s_rstd[w], b + 1)
                if w == 2:
                    wait(dve, s_xT[2], b)
                elif w == 1:
                    wait(dve, s_xT[3], b - 2)
                else:
                    wait(dve, s_xT[1], min(b + 3, B) if isinstance(b, int) else b + 3)
                for t in range(NT):
                    ins = dve.tensor_scalar(xn[:, w % 2, t, :], src[:, t, :], meanvar[:, w - 1, t, 0:1],
                                            rstd[:, w - 1, t:t + 1], ALU.subtract, ALU.mult)
                ins.then_inc(s_xn[w], 1)

            spike_ops = 3 * (STEPS - 1) + 1

            def spike_step(w, b, n):
                base = b * spike_ops
                if n < 2:
                    dve.wait_ge(s_ysb[w], b * 2 + 2)
                else:
                    dve.wait_ge(s_spk[w], base + (n if n % 3 != 1 else n - 1))
                mem, sign, fires = (ysb, 1.0, ALU.is_gt) if n < 3 else (negmem, -1.0, ALU.is_lt)
                if n == 0:
                    ins = dve.tensor_scalar(spikes[:, :], mem[:, :], THRESHOLD, None, fires)
                elif n % 3 == 0:
                    ins = dve.scalar_tensor_tensor(out=spikes[:, :], in0=mem[:, :], scalar=sign * THRESHOLD, in1=spikes[:, :],
                                                   op0=fires, op1=ALU.add)
                elif n % 3 == 1:
                    ins = dve.scalar_tensor_tensor(out=drive[:, :], in0=mem[:, :], scalar=sign * BETA, in1=ysb[:, :],
                                                   op0=ALU.mult, op1=ALU.add)
                else:
                    ins = dve.scalar_tensor_tensor(out=negmem[:, :], in0=mem[:, :], scalar=sign * THRESHOLD, in1=drive[:, :],
                                                   op0=fires, op1=ALU.subtract)
                ins.then_inc(s_spk[w], 1)

            def add_spikes(dst, src, w, b, done):
                dve.wait_ge(s_spk[w], b * spike_ops + spike_ops)
                dve.scalar_tensor_tensor(out=dst, in0=spikes[:, :].rearrange("p (t c) -> p t c", c=C), scalar=0.5 / STEPS,
                                         in1=src, op0=ALU.mult, op1=ALU.add).then_inc(done, 1)

            def finish1(b, par):
                add_spikes(x1[:, :, :], x_in[:, par, :, :], 1, b, s_x1)

            def stats2(b, par):
                dve.wait_ge(s_x1, b + 1)
                stats_of(2, x1, b)
                for t in range(NT):
                    ins = dve.tensor_tensor(x1b[:, par, t, :], x1[:, t, :], bias[:, :], ALU.add)
                ins.then_inc(s_x1b, 1)

            def residual2(n, t, b, par):
                dve.wait_ge(s_out, b * NT + (t + 1))
                if t == 0:
                    dve.wait_ge(s_x1b, b + 1)
                dve.tensor_tensor(x2[:, t, :], side_bank[n % 2][:, 0:C], x1b[:, par, t, :], ALU.add).then_inc(s_x2, 1)

            def stats3(b):
                dve.wait_ge(s_x2, b * NT + NT)
                stats_of(3, x2, b)

            def finish3(b):
                wait(dve, s_stored, b * 16)
                add_spikes(x3[:, :, :], x2[:, :, :], 3, b, s_x3)

            def low_half(n, kind, i, b, s, par):
                src = side_bank[n % 2][:, :]
                if kind == "g":
                    p = (s + 1) % PAIRS
                    dve.wait_ge(s_ghi, g_no(b, p, i))
                    dve.tensor_tensor(g_lo[:, p % 2, i, :], src, g_hi[:, p % 2, i, :].bitcast(F32),
                                      ALU.subtract).then_inc(s_glo, 1)
                elif kind in ("t1", "t2", "t3"):
                    w = int(kind[1])
                    dve.wait_ge(s_xhi[w], b + 1)
                    hi, lo = (xa_hi[:, par, :], xa_lo[:, par, :]) if w == 2 else (xf_hi[:, :], xf_lo[:, :])
                    dve.tensor_tensor(lo, src, hi.bitcast(F32), ALU.subtract).then_inc(s_xlo[w], 1)
                elif kind == "out":
                    residual2(n, i, b, par)

            def steps(b, s, k, par, offsets):
                if 1 in offsets:
                    nb, npar = b + 1, 1 - par
                    if (s, k) == LN1["stats"]:
                        dve.wait_ge(s_xin[npar], (nb - npar) * 8 + 16)
                        stats_of(1, x_in[:, npar, :, :], nb)
                    if (s, k) == LN1["normalise"]:
                        normalise(1, x_in[:, npar, :, :], nb)
                    for n in range(spike_ops):
                        if (s, k) == SPIKE1[n]:
                            spike_step(1, nb, n)
                    if (s, k) == SPIKE1[spike_ops]:
                        finish1(nb, npar)
                    if (s, k) == LN2["stats"]:
                        stats2(nb, npar)
                    if (s, k) == LN2["normalise"]:
                        normalise(2, x1, nb)
                if -1 in offsets:
                    if (s, k) == LN3["stats"]:
                        stats3(b - 1)
                    if (s, k) == LN3["normalise"]:
                        normalise(3, x2, b - 1)
                    for n in range(spike_ops):
                        if (s, k) == SPIKE3[n]:
                            spike_step(3, b - 1, n)
                    if (s, k) == SPIKE3[spike_ops]:
                        finish3(b - 1)

            AGGREGATE = [(LN1["aggregate"], 1, 1), (LN3["aggregate"], 3, -1), (LN2["aggregate"], 2, 1)]

            def slot(b, s, par, offsets):
                for k in range(BEATS):
                    for at, w, off in AGGREGATE:
                        if at == (s, k) and off in offsets:
                            dve.wait_ge(s_stats[w], b + off + 1)
                    if exists(b, s):
                        bias_wait(b, s, k)
                    last = (b, s, k - 2) if k >= 2 else (*before(b, s, 1), BEATS + k - 2)
                    if exists(*last[:2]):
                        recip(*last)
                    if exists(b, s):
                        bias_max(b, s, k)
                    for at, w, off in AGGREGATE:
                        if at == (s, k) and off in offsets:
                            aggregate(w, b + off)
                    for n, kind, i, off, ss in side_at(s, k - 1, offsets):
                        low_half(n, kind, i, b + off, ss, (par + off) % 2)
                    steps(b, s, k, par, offsets)

            def number(kind, i=0):
                return [n for n, x in enumerate(SIDE) if x[2:4] == (kind, i)][0]

            def head():
                qkT = w_qkT.rearrange("p t m c -> p (t m c)")
                for m in range(4):
                    dve.wait_ge(s_wT, m + 1)
                    dve.tensor_copy(qkT[:, m * 512:(m + 1) * 512], banks[m][:, :]).then_inc(s_wTcopied, 1)
                dve.wait_ge(s_wT, 5)
                dve.tensor_copy(wfc_hi[:, :], banks[4][:, :]).then_inc(s_split, 1)
                dve.wait_ge(s_split, 1)
                dve.tensor_tensor(wfc_lo[:, :], banks[4][:, :], wfc_hi[:, :].bitcast(F32), ALU.subtract).then_inc(s_wTcopied, 1)
                dve.wait_ge(s_wT, 6)
                dve.tensor_copy(wproj[:, :, :].rearrange("p t c -> p (t c)"), banks[5][:, :]).then_inc(s_wTcopied, 1)
                for odd in range(2):
                    for half in range(2):
                        n = 2 * odd + half
                        dve.wait_ge(s_a, n + 1)
                        src = banks[(6, 0)[odd] + half][:, :].rearrange("p (m c) -> p m c", c=C)
                        heads = slice(8 * half + odd, 8 * half + odd + 7, 2)
                        dve.tensor_scalar(a_hi[:, heads, :], src, -SCALE, None, ALU.mult).then_inc(s_split, 1)
                        dve.wait_ge(s_split, n + 2)
                        dve.scalar_tensor_tensor(out=a_lo[:, heads, :], in0=src, scalar=-SCALE,
                                                 in1=a_hi[:, heads, :].bitcast(F32), op0=ALU.mult,
                                                 op1=ALU.subtract).then_inc(s_acopied, 1)
                dve.tensor_copy(wv_hi[:, :], w_raw[:, 2 * INNER:3 * INNER]).then_inc(s_split, 1)
                dve.wait_ge(s_split, 6)
                dve.tensor_tensor(wv_lo[:, :], w_raw[:, 2 * INNER:3 * INNER], wv_hi[:, :].bitcast(F32),
                                  ALU.subtract).then_inc(s_split, 1)
                dve.wait_ge(s_split, 7)
                dve.wait_ge(s_xin[0], 16)
                stats_of(1, x_in[:, 0, :, :], 0)
                dve.wait_ge(s_stats[1], 1)
                aggregate(1, 0)
                dve.wait_ge(s_const, 3)
                for h in range(HEADS):
                    ins = dve.tensor_scalar(alibi[:, h, :], dist, SLOPES[h], None, ALU.mult)
                ins.then_inc(s_alibi, 1)
                normalise(1, x_in[:, 0, :, :], 0)
                low_half(number("t1"), "t1", 0, 0, 0, 0)
                for n in range(spike_ops):
                    spike_step(1, 0, n)
                finish1(0, 0)
                stats2(0, 0)
                dve.wait_ge(s_stats[2], 1)
                aggregate(2, 0)
                normalise(2, x1, 0)
                low_half(number("t2"), "t2", 0, 0, 0, 0)
                for h in range(2):
                    low_half(len(SIDE) - 2 + h, "g", h, 0, PAIRS - 1, 0)
                dve.wait_ge(s_alibi, 1)

            def tail():
                for s in range(2):
                    slot(B, s, B % 2, ())
                b = B - 1
                for t in range(NT):
                    low_half(number("out", t), "out", t, b, 0, b % 2)
                stats3(b)
                dve.wait_ge(s_stats[3], b + 1)
                aggregate(3, b)
                normalise(3, x2, b)
                low_half(number("t3"), "t3", 0, b, 0, b % 2)
                for n in range(spike_ops):
                    spike_step(3, b, n)
                finish3(b)

            run(dve, slot, head, tail)

        @block.scalar
        def _(act):
            def exps(b, p, k):
                act.wait_ge(s_biased, tile_no(b, p, k))
                if k == 0:
                    bb, pp = before(b, p, 2)
                    wait(act, s_turned, turn_no(bb, pp, len(TRUNS) - 1))
                col = 0
                for h, i in TILES[k]:
                    seg = SEG[h, i]
                    ins = act.activation(prob[:, p % 2, h, PCOL[i]:PCOL[i] + WIDTH[i]], negsc[:, k % 3, col:col + WIDTH[i]],
                                         ACT.Exp, bias=negmax[:, p % 2, seg:seg + 1], scale=-1.0,
                                         accum_out=sums[:, p % 2, seg:seg + 1])
                    col += WIDTH[i]
                ins.then_inc(s_exp, 1)

            def turned_out(b, p, t):
                act.wait_ge(s_turned, turn_no(b, p, t))
                if t == 0:
                    bb, pp = before(b, p, 2)
                    wait(act, s_pv, pair_no(bb, pp))
                act.copy(probT[:, p % 2, t, :], turn_bank[(len(TRUNS) * p + t) % 2][:, :]).then_inc(s_turned_out, 1)

            def att_out(b, p, par):
                act.wait_ge(s_pv, pair_no(b, p))
                if p == 2:
                    wait(act, s_out, b * NT)
                act.copy(attT[:, att_at(p, par), :], pv_bank[:, :]).then_inc(s_att, 1)

            def high_half(n, kind, i, b, s, par):
                src = side_bank[n % 2][:, :]
                if kind == "g":
                    p = (s + 1) % PAIRS
                    act.wait_ge(s_g, g_no(b, p, i))
                    act.copy(g_hi[:, p % 2, i, :], src).then_inc(s_ghi, 1)
                elif kind == "v":
                    q = s // 2
                    act.wait_ge(s_v, v_no(b, q, i))
                    wait(act, s_pv, pair_no(b, 2 * q - 3))
                    act.copy(vals[:, q % 2, 2 * i:2 * i + 2, :], src.rearrange("p (t n) -> p t n", t=2)).then_inc(s_vals, 1)
                elif kind in ("t1", "t2", "t3"):
                    w = int(kind[1])
                    act.wait_ge(s_xT[w], b + 1)
                    hi = xa_hi[:, par, :] if w == 2 else xf_hi[:, :]
                    if w == 1:
                        wait(act, s_fc[3], (b - 2) * FC)
                    if w == 3:
                        wait(act, s_fc[1], (b + 2) * FC + FC if not isinstance(b, int) else (min(b + 2, B - 1) + 1) * FC)
                    act.copy(hi, src).then_inc(s_xhi[w], 1)
                elif kind in ("fc1", "fc3"):
                    w = int(kind[2])
                    act.wait_ge(s_fc[w], b * FC + (i + 1))
                    if i >= 2:
                        act.wait_ge(s_hid[w], b * FC + (i - 1))
                    act.activation(relu[:, i % 2, :], src, ACT.Relu).then_inc(s_relu[w], 1)
                elif kind in ("y1", "y3"):
                    w = int(kind[1])
                    act.wait_ge(s_y[w], b * 2 + (i + 1))
                    if w == 1:
                        wait(act, s_x3, b - 2)
                    else:
                        wait(act, s_x1, b + 3 if not isinstance(b, int) else min(b + 3, B))
                    act.copy(ysb[:, i * 2 * C:(i + 1) * 2 * C], src[:, 0:2 * C]).then_inc(s_ysb[w], 1)

            def slot(b, s, par, offsets):
                for k in range(BEATS):
                    for n, kind, i, off, ss in side_at(s, k - 1, offsets):
                        high_half(n, kind, i, b + off, ss, (par + off) % 2)
                    if k == ATTBEAT and exists(*before(b, s, 2)):
                        att_out(*before(b, s, 2), par if s >= 2 else 1 - par)
                    if exists(b, s):
                        exps(b, s, k)
                    for t in range(len(TRUNS)):
                        if TBEAT[t] == k and exists(*before(b, s, 1)):
                            turned_out(*before(b, s, 1), t)

            def chain(b, names):
                for n, (s, _, kind, i, off) in enumerate(SIDE):
                    if kind in names:
                        high_half(n, kind, i, b, s, b % 2)

            def head():
                chain(0, ("t1", "fc1", "y1", "t2"))
                for h in range(2):
                    high_half(len(SIDE) - 2 + h, "g", h, 0, PAIRS - 1, 0)

            def tail():
                for s in range(2):
                    slot(B, s, B % 2, ())
                chain(B - 1, ("t3", "fc3", "y3"))

            run(act, slot, head, tail)

        @block.gpsimd
        def _(pool):
            def norm(b, p, k):
                pool.wait_ge(s_rsum, tile_no(b, p, k))
                for h, i in TILES[k]:
                    seg = SEG[h, i]
                    pr = prob[:, p % 2, h, PCOL[i]:PCOL[i] + WIDTH[i]]
                    ins = pool.tensor_tensor(pr, pr, rsum[:, p % 2, seg:seg + 1].to_broadcast([P, WIDTH[i]]), ALU.mult)
                ins.then_inc(s_norm, 1)

            def square(w, i, b, offsets=(1,)):
                pool.wait_ge(s_relu[w], b * FC + (i + 1))
                if i == 0:
                    if w == 1:
                        wait(pool, s_y[3], (b - 2) * 2)
                    else:
                        wait(pool, s_y[1], (b + 3 if not isinstance(b, int) else min(b + 3, B)) * 2)
                pool.tensor_tensor(hid[:, i, :], relu[:, i % 2, :], relu[:, i % 2, :], ALU.mult).then_inc(s_hid[w], 1)

            def inverse_std(w, b):
                pool.wait_ge(s_mv[w], b + 1)
                pool.tensor_tensor(vareps[:, w - 1, :], meanvar[:, w - 1, :, 1], eps[:, :], ALU.add).then_inc(s_ve[w], 1)
                pool.wait_ge(s_ve[w], b + 1)
                pool.tensor_tensor(rstd[:, w - 1, :], vareps[:, w - 1, :], minus_half[:, :], ALU.pow).then_inc(s_rstd[w], 1)

            def slot(b, s, par, offsets):
                for k in range(BEATS):
                    last = (b, s, k - 2) if k >= 2 else (*before(b, s, 1), BEATS + k - 2)
                    if exists(*last[:2]):
                        norm(*last)
                    for n, kind, i, off, _ in side_at(s, k - 1, offsets):
                        if kind in ("fc1", "fc3"):
                            square(int(kind[2]), i, b + off)
                    for at, w, off in ((LN1["rstd"], 1, 1), (LN3["rstd"], 3, -1), (LN2["rstd"], 2, 1)):
                        if at == (s, k) and off in offsets:
                            inverse_std(w, b + off)

            def head():
                pool.memset(ident[:, :], 0.0).then_inc(s_const0, 1)
                pool.iota(dist, pattern=[[-1, N]], base=N - P, channel_multiplier=1,
                          allow_small_or_imprecise_dtypes=True).then_inc(s_dist0, 1)
                pool.memset(eps[:, :], EPS)
                pool.memset(minus_half[:, :], -0.5).then_inc(s_const, 1)
                pool.wait_ge(s_const0, 1)
                pool.affine_select(out=ident[:, :], in_=ident[:, :], compare_op=ALU.not_equal, fill=1.0, base=0,
                                   pattern=[[-1, P]], channel_multiplier=1).then_inc(s_const, 1)
                pool.wait_ge(s_dist0, 1)
                pool.affine_select(out=dist, in_=dist, compare_op=ALU.is_ge, fill=MASKED, base=N - P,
                                   pattern=[[-1, N]], channel_multiplier=1).then_inc(s_const, 1)
                pool.wait_ge(s_const, 1)
                inverse_std(1, 0)
                for i in range(FC):
                    square(1, i, 0)
                inverse_std(2, 0)

            def tail():
                for s in range(2):
                    slot(B, s, B % 2, ())
                inverse_std(3, B - 1)
                for i in range(FC):
                    square(3, i, B - 1)

            run(pool, slot, head, tail)


_INS = ['L0_attn_x', 'L0_attn_w_qkv', 'L0_attn_w_out', 'L0_attn_b_out', 'L0_ffn_W_fc', 'L0_ffn_W_proj']
_OUTS = [((16, 512, 128), 'float32')]


def kernel(**inputs):
    import numpy as _np
    import concourse.bacc as _bacc
    from concourse import mybir as _mybir
    from concourse.bass_utils import run_bass_kernel_spmd as _run

    nc = _bacc.Bacc("TRN2", target_bir_lowering=False, num_devices=1)
    arrays, args = {}, []
    for name in _INS:
        a = _np.ascontiguousarray(inputs[name])
        arrays[f"in_{name}_dram"] = a
        args.append(nc.dram_tensor(f"in_{name}_dram", a.shape, _mybir.dt.from_np(a.dtype), kind="ExternalInput").ap())
    for i, (shape, dtype) in enumerate(_OUTS):
        dt = _mybir.dt.from_np(_np.dtype(dtype))
        args.append(nc.dram_tensor(f"out_{i}_dram", shape, dt, kind="ExternalOutput").ap())
    macaron_kernel(nc, *args)
    r = _run(nc, [arrays], core_ids=[0])
    got = tuple(r.results[0][f"out_{i}_dram"] for i in range(len(_OUTS)))
    return got[0]
```

```python
from contextlib import ExitStack

import concourse.bass as bass
from concourse import mybir

ALU = mybir.AluOpType
ACT = mybir.ActivationFunctionType
F32 = mybir.dt.float32
F32R = mybir.dt.float32r

P = 128
B, N, C = 16, 512, 128
HEADS, DH = 16, 64
F = 4 * C
NT = N // P
FC = F // P
PAIRS = HEADS // 2
INNER = HEADS * DH
SCALE = DH ** -0.5
EPS = 1e-5
BETA, THRESHOLD, STEPS = 0.9, 1.0, 5
SLOPES = [2.0 ** (-0.5 * (h + 1)) for h in range(HEADS)]
MASKED = 3.0e38

TILES = [[(1, 3)], [(1, 2)], [(0, 3)], [(0, 2)], [(1, 1), (0, 1)], [(1, 0), (0, 0)]]
BEATS = len(TILES)
SEG = {hi: n for n, hi in enumerate(x for t in TILES for x in t)}
SEG_TILE = {hi: k for k, t in enumerate(TILES) for hi in t}
WIDTH = [(i + 1) * P for i in range(NT)]
PCOL = [sum(WIDTH[i + 1:]) for i in range(NT)]
PHEAD = sum(WIDTH)
TRUNS = [[(1, 2), (0, 2)], [(1, 1), (1, 3)], [(0, 1), (0, 3)], [(1, 0)], [(0, 0)]]
TNEEDS = [max(SEG_TILE[h, i] for h, j in runs for i in range(j, NT)) for runs in TRUNS]
TRING = 8
TBEAT = [1, 2, 3, 5, 5]
ATTBEAT = 4
PV = [[2], [], [1, 3], [], [0], []]
PVORDER = [j for js in PV for j in js]
PVLAST = [max(PVORDER.index(j) for _, j in runs) for runs in TRUNS]


def place_of(h, j):
    for t, runs in enumerate(TRUNS):
        col = 0
        for hh, jj in runs:
            if (hh, jj) == (h, j):
                return t, col
            col += (NT - jj) * P


def beats_from(slot, beat, counts):
    at = [divmod(slot * BEATS + beat + n, BEATS) for n in range(len(counts))]
    return [x for x, c in zip(at, counts) for _ in range(c)]


SIDE = [
    (0, 0, "q", 0, 0), (0, 1, "k", 0, 0), (0, 3, "v", 0, 0), (0, 4, "t1", 0, 1), (0, 4, "v", 1, 0),
    (1, 0, "q", 0, 0), (1, 1, "k", 0, 0), (1, 2, "fc1", 0, 1), (1, 4, "fc1", 1, 1), (1, 4, "fc1", 2, 1),
    (2, 0, "fc1", 3, 1), (2, 0, "q", 0, 0), (2, 1, "out", 0, -1), (2, 1, "out", 1, -1), (2, 2, "y1", 0, 1),
    (2, 2, "k", 0, 0), (2, 3, "out", 2, -1), (2, 4, "y1", 1, 1), (2, 5, "v", 0, 0),
    (3, 0, "v", 1, 0), (3, 0, "q", 0, 0), (3, 1, "k", 0, 0), (3, 2, "out", 3, -1),
    (4, 0, "k", 0, 0), (4, 0, "q", 0, 0), (4, 2, "t3", 0, -1), (4, 3, "v", 0, 0), (4, 4, "v", 1, 0),
    (5, 0, "q", 0, 0), (5, 1, "fc3", 0, -1), (5, 2, "k", 0, 0), (5, 4, "fc3", 1, -1), (5, 4, "fc3", 2, -1),
    (5, 5, "fc3", 3, -1),
    (6, 0, "q", 0, 0), (6, 1, "k", 0, 0), (6, 2, "y3", 0, -1), (6, 2, "y3", 1, -1), (6, 3, "t2", 0, 1),
    (6, 4, "v", 0, 0), (6, 5, "v", 1, 0),
    (7, 0, "q", 0, 1), (7, 1, "k", 0, 1),
]
SPIKE1 = beats_from(3, 0, [2, 3, 1, 1, 0, 0, 1, 1, 1, 1, 2, 1])
SPIKE3 = beats_from(6, 3, [1, 2, 2, 1, 2, 1, 2, 1, 2])
LN1 = dict(stats=(0, 0), aggregate=(0, 1), rstd=(0, 1), normalise=(0, 3))
LN2 = dict(stats=(5, 2), aggregate=(5, 3), rstd=(5, 3), normalise=(6, 1))
LN3 = dict(stats=(3, 4), aggregate=(3, 5), rstd=(3, 5), normalise=(4, 0))


def macaron_kernel(nc: bass.Bass, x, w_qkv, w_out, b_out, w_fc, w_proj, out):
    ctx = ExitStack()
    with ctx:
        def sb(name, shape, dt=F32):
            return ctx.enter_context(nc.sbuf_tensor(name, shape, dt))

        def sem(name):
            return ctx.enter_context(nc.semaphore(name))

        banks = [ctx.enter_context(nc.psum_tensor(f"bank{i}", [P, 512], F32)) for i in range(8)]
        score_bank, turn_bank, pv_bank, side_bank = banks[0:3], banks[3:5], banks[5], banks[6:8]
        last_out_bank = side_bank + score_bank[0:2]

        ident = sb("ident", [P, P])
        minus_half = sb("minus_half", [P, NT])
        eps = sb("eps", [P, NT])
        alibi = sb("alibi", [P, HEADS, N])
        wq_hi = sb("wq_hi", [P, INNER], F32R)
        wq_lo = sb("wq_lo", [P, INNER], F32R)
        wk_hi = sb("wk_hi", [P, INNER], F32R)
        wk_lo = sb("wk_lo", [P, INNER], F32R)
        wv_hi = sb("wv_hi", [P, INNER], F32R)
        wv_lo = sb("wv_lo", [P, INNER], F32R)
        wo = sb("wo", [P, PAIRS, C])
        wfc_hi = sb("wfc_hi", [P, F], F32R)
        wfc_lo = sb("wfc_lo", [P, F], F32R)
        wproj = sb("wproj", [P, FC, C])
        bias = sb("bias", [P, C])
        x_in = sb("x_in", [P, 2, NT, C])
        x1b = sb("x1b", [P, 2, NT, C])
        x1 = sb("x1", [P, NT, C])
        x2 = sb("x2", [P, NT, C])
        x3 = sb("x3", [P, NT, C])
        xn = sb("xn", [P, NT, C])
        stats = sb("stats", [P, 3, NT, 6])
        meanvar = sb("meanvar", [P, 3, NT, 2])
        vareps = sb("vareps", [P, 3, NT])
        rstd = sb("rstd", [P, 3, NT])
        xf_hi = sb("xf_hi", [P, N], F32R)
        xf_lo = sb("xf_lo", [P, N], F32R)
        xa_hi = sb("xa_hi", [P, 2, N], F32R)
        xa_lo = sb("xa_lo", [P, 2, N], F32R)
        hid = sb("hid", [P, FC, N])
        ysb = sb("ysb", [P, N])
        negmem = sb("negmem", [P, N])
        drive = sb("drive", [P, N])
        spikes = sb("spikes", [P, N])
        queries = sb("queries", [P, 2, 2, 2, N], F32R)
        q_hi, q_lo = queries[:, :, :, 0, :], queries[:, :, :, 1, :]
        keys = sb("keys", [P, 2, 2, N], F32R)
        k_lo = sb("k_lo", [P, N], F32R)
        vals = sb("vals", [P, 2, NT, 4 * DH])
        negsc = sb("negsc", [P, 3, N])
        negmax = sb("negmax", [P, 2, 8])
        sums = sb("sums", [P, 2, 8])
        rsum = sb("rsum", [P, 2, 8])
        prob = sb("prob", [P, 2, 2, PHEAD])
        probT = sb("probT", [P, TRING, N])
        attT = sb("attT", [P, PAIRS + 2, N])
        w_raw = prob[:, :, :, :].rearrange("p a h n -> p (a h n)")[:, 0:3 * INNER]
        dist = probT[:, 5, :]
        fc_raw, proj_raw = probT[:, 0, :], probT[:, 1, :]

        s_wfc, s_wproj, s_wqkv, s_wo, s_stored = (sem(n) for n in ("s_wfc", "s_wproj", "s_wqkv", "s_wo", "s_stored"))
        s_keys = [[sem(f"s_keys_{n}{h}") for h in range(2)] for n in ("even", "odd")]
        s_twice = [[sem(f"s_twice_{n}{h}") for h in range(2)] for n in ("even", "odd")]
        s_xin = [sem("s_xin_even"), sem("s_xin_odd")]
        s_const, s_const0, s_dist0, s_wT = (sem(n) for n in ("s_const", "s_const0", "s_dist0", "s_wT"))
        s_wfc_hi, s_wfc_lo, s_wproj_out, s_whi, s_wlo, s_alibi = (
            sem(n) for n in ("s_wfc_hi", "s_wfc_lo", "s_wproj_out", "s_whi", "s_wlo", "s_alibi"))
        s_scores, s_biased, s_exp, s_rsum, s_norm = (sem(n) for n in ("s_scores", "s_biased", "s_exp", "s_rsum", "s_norm"))
        s_turned, s_turned_out, s_pv, s_att = (sem(n) for n in ("s_turned", "s_turned_out", "s_pv", "s_att"))
        s_q, s_qhi, s_qlo, s_k, s_khi, s_klo, s_v, s_vals = (
            sem(n) for n in ("s_q", "s_qhi", "s_qlo", "s_k", "s_khi", "s_klo", "s_v", "s_vals"))
        s_fc, s_relu, s_hid, s_y, s_ysb, s_spk = (
            {w: sem(f"{n}{w}") for w in (1, 3)} for n in ("s_fc", "s_relu", "s_hid", "s_y", "s_ysb", "s_spk"))
        s_stats, s_mv, s_ve, s_rstd, s_xn, s_xT, s_xhi, s_xlo = (
            {w: sem(f"{n}{w}") for w in (1, 2, 3)}
            for n in ("s_stats", "s_mv", "s_ve", "s_rstd", "s_xn", "s_xT", "s_xhi", "s_xlo"))
        s_spk_half = [sem("s_spk_first"), sem("s_spk_second")]
        s_out, s_x1, s_x1b, s_x2, s_x3 = (sem(n) for n in ("s_out", "s_x1", "s_x1b", "s_x2", "s_x3"))

        def wait(eng, semaphore, value):
            if not isinstance(value, int) or value > 0:
                eng.wait_ge(semaphore, value)

        def tile_no(b, p, k):
            return b * (PAIRS * BEATS) + (p * BEATS + k + 1)

        def turn_no(b, p, t):
            return b * (PAIRS * len(TRUNS)) + (p * len(TRUNS) + t + 1)

        def pair_no(b, p):
            return b * PAIRS + (p + 1)

        def twice_no(b, p, h):
            return (b * (PAIRS // 2) + (p // 2 + 1)) * (16, 32)[h]

        def keys_no(b, p, h):
            return (b * (PAIRS // 2) + (p // 2 + 1)) * (16, 32)[h]

        def pv_no(b, p, n):
            return b * (PAIRS * NT) + (p * NT + n + 1)

        def turn_slot(p, t):
            return (len(TRUNS) * p + t) % TRING

        def score_col(k, n):
            return n * 2 * P

        def v_no(b, q, i):
            return b * PAIRS + (2 * q + i + 1)

        def before(b, p, back):
            return (b, p - back) if p >= back else (b - 1, p - back + PAIRS)

        def exists(b, p):
            return not isinstance(b, int) or (0 <= b < B)

        def freed(kind, i, b, s):
            if kind in "qk":
                p = (s + 1) % PAIRS
                return (s_qlo if kind == "q" else s_klo), pair_no(b, p)
            if kind == "v":
                return s_vals, v_no(b, s // 2, i)
            if kind in ("t1", "t2", "t3"):
                return s_xlo[int(kind[1])], b + 1
            if kind in ("fc1", "fc3"):
                return s_relu[int(kind[2])], b * FC + (i + 1)
            if kind in ("y1", "y3"):
                return s_ysb[int(kind[1])], b * 2 + (i + 1)
            return s_x2, b * NT + (i + 1)

        def last_user(n, b, offsets):
            for m in range(n - 1, -1, -1):
                s, _, kind, i, off = SIDE[m]
                if m % 2 == n % 2 and off in offsets:
                    return freed(kind, i, b + off, s)
            m = len(SIDE) - 1 - (len(SIDE) - 1 - n) % 2
            s, _, kind, i, off = SIDE[m]
            assert kind in "qk"
            return freed(kind, i, b - 1 + off, s)

        def att_at(p, par):
            return PAIRS + p if p < 2 and par else p

        def run(eng, slot, head, tail):
            head()
            for s in range(PAIRS):
                slot(0, s, 0, (0, 1))
            with eng.Fori(1, B - 1, 2) as b:
                for ahead in range(2):
                    for s in range(PAIRS):
                        slot(b + ahead, s, (1 + ahead) % 2, (-1, 0, 1))
            for s in range(PAIRS):
                slot(B - 1, s, (B - 1) % 2, (-1, 0))
            tail()

        def side_at(s, k, offsets):
            s, k = (s, k) if k >= 0 else (s - 1, BEATS - 1)
            return [(n, kind, i, off, s) for n, (ss, kk, kind, i, off) in enumerate(SIDE)
                    if (ss, kk) == (s, k) and off in offsets]

        block = ctx.enter_context(nc.Block())

        @block.sync
        def _(sp):
            xt = x.rearrange("b (t p) c -> b p t c", p=P)
            ot = out.rearrange("b (t p) c -> b p t c", p=P)

            def load_x(b, par):
                wait(sp, s_x1, b - 1)
                sp.dma_start(x_in[:, par, :, :], xt[b] if isinstance(b, int) else
                             xt[bass.ds(b, 1)].rearrange("b p t c -> (b p) t c")).then_inc(s_xin[par], 16)

            def store_x(b):
                wait(sp, s_x3, b + 1)
                sp.dma_start(ot[b] if isinstance(b, int) else
                             ot[bass.ds(b, 1)].rearrange("b p t c -> (b p) t c"), x3[:, :, :]).then_inc(s_stored, 16)

            def place(b, p):
                top, low = slice(0, DH), slice(DH, P)
                par = p % 2
                sp.wait_ge(s_qlo, pair_no(b, p))
                for rows in (top, low):
                    sp.dma_start(queries[rows, par, 1, :, :].bitcast(F32),
                                 queries[low, par, 0, :, :].bitcast(F32)).then_inc(s_twice[par][1], 16)
                sp.wait_ge(s_khi, pair_no(b, p))
                sp.dma_start(keys[top, par, 1, :].bitcast(F32), keys[low, par, 0, :].bitcast(F32)).then_inc(s_keys[par][1], 16)
                sp.wait_ge(s_klo, pair_no(b, p))
                sp.dma_start(keys[low, par, 1, :].bitcast(F32), k_lo[low, :].bitcast(F32)).then_inc(s_keys[par][1], 16)
                sp.wait_ge(s_twice[par][1], twice_no(b, p, 1))
                sp.dma_start(queries[low, par, 0, :, :].bitcast(F32),
                             queries[top, par, 0, :, :].bitcast(F32)).then_inc(s_twice[par][0], 16)
                sp.wait_ge(s_keys[par][1], keys_no(b, p, 1))
                sp.dma_start(keys[low, par, 0, :].bitcast(F32), k_lo[top, :].bitcast(F32)).then_inc(s_keys[par][0], 16)

            def slots(b, par, last):
                if last >= 2:
                    load_x(b + 2, par)
                for s in range(PAIRS):
                    if s < PAIRS - 1 or last >= 1:
                        place(*((b, s + 1) if s < PAIRS - 1 else (b + 1, 0)))
                if not isinstance(b, int) or b > 0:
                    store_x(b - 1)

            load_x(0, 0)
            sp.dma_start(fc_raw.rearrange("p (t c) -> p t c", c=C), w_fc.rearrange("(t p) c -> p t c", p=P)).then_inc(s_wfc, 16)
            sp.dma_start(proj_raw, w_proj).then_inc(s_wproj, 16)
            sp.dma_start(w_raw, w_qkv).then_inc(s_wqkv, 16)
            sp.dma_start(bias[:, :], b_out.rearrange("(a c) -> a c", a=1).to_broadcast([P, C])).then_inc(s_wo, 16)
            sp.dma_start(wo[:, :, :], w_out.rearrange("(m p) c -> p m c", p=P)).then_inc(s_wo, 16)
            load_x(1, 1)
            place(0, 0)
            slots(0, 0, 2)
            with sp.Fori(1, B - 3, 2) as b:
                for ahead in range(2):
                    slots(b + ahead, (1 + ahead) % 2, 2)
            for b in range(B - 3, B):
                slots(b, b % 2, min(2, B - 1 - b))
            store_x(B - 1)
            sp.wait_ge(s_stored, 16 * B)

        @block.tensor
        def _(pe):
            def product3(dst, w_hi, w_lo, m_hi, m_lo):
                pe.matmul(dst, w_hi, m_hi, start=True, stop=False)
                pe.matmul(dst, w_hi, m_lo, start=False, stop=False)
                return pe.matmul(dst, w_lo, m_hi, start=False, stop=True)

            def scores(b, p, k, par):
                first, i = TILES[k][0]
                if i == NT - 1:
                    pe.wait_ge(s_twice[p % 2][first], twice_no(b, p, first))
                    pe.wait_ge(s_keys[p % 2][first], keys_no(b, p, first))
                wait(pe, s_biased, tile_no(b, p, k - 3))
                rows = slice(i * P, (i + 1) * P)
                width = max(WIDTH[i], 2 * P)
                for n, (h, _) in enumerate(TILES[k]):
                    dst = score_bank[k % 3][:, score_col(k, n):score_col(k, n) + width]
                    pe.matmul(dst, q_hi[:, p % 2, h, rows], keys[:, p % 2, h, 0:width], start=True, stop=False)
                    mm = pe.matmul(dst, q_lo[:, p % 2, h, rows], keys[:, p % 2, h, 0:width], start=False, stop=True)
                mm.then_inc(s_scores, 1)

            def turn(b, p, t):
                pe.wait_ge(s_norm, tile_no(b, p, TNEEDS[t]))
                n = len(TRUNS) * p + t
                bb, pp = before(b, p, 1)
                prev = turn_no(b, p, t - 2)
                wait(pe, s_turned_out, prev)
                col = 0
                for h, j in TRUNS[t]:
                    for i in range(j, NT):
                        mm = pe.transpose(turn_bank[n % 2][:, col:col + P],
                                          prob[:, p % 2, h, PCOL[i] + j * P:PCOL[i] + (j + 1) * P], ident[:, :])
                        col += P
                mm.then_inc(s_turned, 1)

            def pv(b, p, j):
                tiles = [place_of(h, j) for h in range(2)]
                pe.wait_ge(s_turned_out, turn_no(b, p, max(t for t, _ in tiles)))
                if j == PVORDER[0]:
                    pe.wait_ge(s_vals, v_no(b, p // 2, 1))
                    wait(pe, s_att, pair_no(b, p - 1))
                for h in range(2):
                    t, col = tiles[h]
                    width = (NT - j) * P
                    mm = pe.matmul(pv_bank[h * DH:(h + 1) * DH, j * P:N],
                                   vals[:, (p // 2) % 2, j, (p % 2) * P + h * DH:(p % 2) * P + (h + 1) * DH],
                                   probT[:, turn_slot(p, t), col:col + width], start=(j == PVORDER[0]),
                                   stop=(j == PVORDER[-1]), skip_group_check=True)
                mm.then_inc(s_pv, 1)

            def qk_tile(dst, kind, b, p, par):
                if (p, kind) == (0, "q"):
                    pe.wait_ge(s_xlo[2], b + 1)
                hi, lo, done = (wq_hi, wq_lo, s_q) if kind == "q" else (wk_hi, wk_lo, s_k)
                cols = slice(p * P, (p + 1) * P)
                product3(dst, hi[:, cols], lo[:, cols], xa_hi[:, par, :], xa_lo[:, par, :]).then_inc(done, 1)

            def v_tile(dst, q, i, par):
                for n in range(2):
                    rows = slice((2 * i + n) * P, (2 * i + n + 1) * P)
                    cols = slice(q * 4 * DH, (q + 1) * 4 * DH)
                    mm = product3(dst[:, n * 4 * DH:(n + 1) * 4 * DH], xa_hi[:, par, rows], xa_lo[:, par, rows],
                                  wv_hi[:, cols], wv_lo[:, cols])
                mm.then_inc(s_v, 1)

            def norm_turn(dst, w, b):
                pe.wait_ge(s_xn[w], b + 1)
                for t in range(NT):
                    mm = pe.transpose(dst[:, t * P:(t + 1) * P], xn[:, t, :], ident[:, :])
                mm.then_inc(s_xT[w], 1)

            def fc_tile(dst, w, i, b):
                if i == 0:
                    pe.wait_ge(s_xlo[w], b + 1)
                rows = slice(i * P, (i + 1) * P)
                product3(dst, wfc_hi[:, rows], wfc_lo[:, rows], xf_hi[:, :], xf_lo[:, :]).then_inc(s_fc[w], 1)

            def y_tile(dst, w, half, b):
                for i in range(FC):
                    pe.wait_ge(s_hid[w], b * FC + (i + 1))
                    for t in range(2):
                        rows = slice((2 * half + t) * P, (2 * half + t + 1) * P)
                        mm = pe.matmul(dst[:, t * C:(t + 1) * C], hid[:, i, rows], wproj[:, i, :],
                                       start=(i == 0 and t == 0), stop=(i == FC - 1), skip_group_check=True)
                mm.then_inc(s_y[w], 1)

            def out_tile(dst, t, b, par):
                pe.wait_ge(s_att, pair_no(b, PAIRS - 1))
                for m in range(PAIRS):
                    mm = pe.matmul(dst[:, 0:C], attT[:, att_at(m, par), t * P:(t + 1) * P], wo[:, m, :],
                                   start=(m == 0), stop=(m == PAIRS - 1))
                mm.then_inc(s_out, 1)

            def last_out(t, pairs, par):
                for m in pairs:
                    mm = pe.matmul(last_out_bank[t][:, 0:C], attT[:, att_at(m, par), t * P:(t + 1) * P], wo[:, m, :],
                                   start=(m == 0), stop=(m == PAIRS - 1), skip_group_check=True)
                if pairs[-1] == PAIRS - 1:
                    mm.then_inc(s_out, 1)

            def side(n, kind, i, off, b, s, par, last):
                if last:
                    wait(pe, *last)
                dst = side_bank[n % 2][:, :]
                b, par = b + off, (par + off) % 2
                if kind in "qk":
                    qk_tile(dst, kind, b, (s + 1) % PAIRS, par)
                elif kind == "v":
                    v_tile(dst, s // 2, i, par)
                elif kind in ("t1", "t2", "t3"):
                    norm_turn(dst, int(kind[1]), b)
                elif kind in ("fc1", "fc3"):
                    fc_tile(dst, int(kind[2]), i, b)
                elif kind in ("y1", "y3"):
                    y_tile(dst, int(kind[1]), i, b)
                else:
                    out_tile(dst, i, b, par)

            def keep_warm(count):
                for _ in range(count):
                    pe.matmul(pv_bank[:, 0:P], ident[:, :], ident[:, :], start=True, stop=True)

            def slot(b, s, par, offsets, between=None):
                t_of, pv_of = before(b, s, 1), before(b, s, 2)
                for k in range(BEATS):
                    if exists(b, s):
                        scores(b, s, k, par)
                    for j in PV[k]:
                        if exists(*pv_of):
                            pv(*pv_of, j)
                    for t in range(len(TRUNS)):
                        if TBEAT[t] == k and exists(*t_of):
                            turn(*t_of, t)
                    for n, kind, i, off, _ in side_at(s, k, offsets):
                        side(n, kind, i, off, b, s, par, last_user(n, b, offsets))
                    if between:
                        between(k)

            def chain(b, names, users=None):
                tiles = [(n, s, kind, i) for n, (s, _, kind, i, off) in enumerate(SIDE) if kind in names]
                users = dict(users or {})
                for n, s, kind, i in tiles:
                    side(n, kind, i, 0, b, s, b % 2, users.get(n % 2))
                    users[n % 2] = freed(kind, i, b, s)
                return users

            def head():
                pe.wait_ge(s_const, 2)
                for ready, raw, bank in ((s_wfc, fc_raw, score_bank[0]), (s_wproj, proj_raw, score_bank[1])):
                    pe.wait_ge(ready, 16)
                    for m in range(FC):
                        mm = pe.transpose(bank[:, m * P:(m + 1) * P], raw[:, m * P:(m + 1) * P], ident[:, :])
                    mm.then_inc(s_wT, 1)
                pe.wait_ge(s_wfc_lo, 1)
                users = chain(0, ("t1", "fc1"))
                pe.wait_ge(s_wproj_out, 1)
                users = chain(0, ("y1",), users)
                pe.wait_ge(s_x1, 1)
                keep_warm(9)
                users = chain(0, ("t2",), users)
                pe.wait_ge(s_wlo, 2)
                for n in range(len(SIDE) - 2, len(SIDE)):
                    side(n, SIDE[n][2], 0, 0, 0, PAIRS - 1, 0, users.get(n % 2))
                pe.wait_ge(s_wlo, 3)
                pe.wait_ge(s_wo, 32)
                keep_warm(14)

            def tail():
                b, par = B - 1, (B - 1) % 2

                def early(k):
                    if k == 0:
                        pe.wait_ge(s_att, pair_no(b, PAIRS - 3))
                        wait(pe, s_biased, tile_no(b, PAIRS - 1, BEATS - 1))
                        for n in range(2):
                            wait(pe, *last_user(len(SIDE) - (len(SIDE) - n) % 2, b, (-1, 0)))
                    if k < NT:
                        last_out(k, range(PAIRS - 2), par)

                slot(B, 0, B % 2, (), early)
                slot(B, 1, B % 2, ())
                pe.wait_ge(s_att, pair_no(b, PAIRS - 1))
                for t in range(NT):
                    last_out(t, range(PAIRS - 2, PAIRS), par)
                keep_warm(16)
                chain(b, ("t3", "fc3", "y3"), {n: (s_x2, b * NT + NT) for n in range(2)})

            run(pe, slot, head, tail)

        @block.vector
        def _(dve):
            def bias_wait(b, p, k):
                dve.wait_ge(s_scores, tile_no(b, p, k))

            def bias_max(b, p, k):
                col = 0
                for n, (h, i) in enumerate(TILES[k]):
                    src = score_bank[k % 3][:, score_col(k, n):score_col(k, n) + WIDTH[i]]
                    ins = dve.tensor_tensor_reduce(negsc[:, k % 3, col:col + WIDTH[i]], src,
                                                   alibi[:, 2 * p + h, N - WIDTH[i]:N], 1.0, MASKED, ALU.add, ALU.min,
                                                   negmax[:, p % 2, SEG[h, i]:SEG[h, i] + 1])
                    col += WIDTH[i]
                ins.then_inc(s_biased, 1)

            def recip(b, p, k):
                dve.wait_ge(s_exp, tile_no(b, p, k))
                cols = slice(SEG[TILES[k][0]], SEG[TILES[k][-1]] + 1)
                dve.reciprocal(rsum[:, p % 2, cols], sums[:, p % 2, cols]).then_inc(s_rsum, 1)

            def stats_of(w, src, b):
                for t in range(NT):
                    ins = dve.bn_stats(stats[:, w - 1, t, :], src[:, t, :])
                ins.then_inc(s_stats[w], 1)

            def aggregate(w, b):
                for t in range(NT):
                    ins = dve.bn_aggr(meanvar[:, w - 1, t, :], stats[:, w - 1, t, :])
                ins.then_inc(s_mv[w], 1)

            def normalise(w, src, b):
                dve.wait_ge(s_rstd[w], b + 1)
                if w == 1:
                    wait(dve, s_xT[2], b)
                elif w == 2:
                    dve.wait_ge(s_xT[1], b + 1)
                    wait(dve, s_xT[3], b - 1)
                else:
                    wait(dve, s_xT[1], min(b + 3, B) if isinstance(b, int) else b + 3)
                    wait(dve, s_xT[2], min(b + 2, B) if isinstance(b, int) else b + 2)
                for t in range(NT):
                    ins = dve.tensor_scalar(xn[:, t, :], src[:, t, :], meanvar[:, w - 1, t, 0:1],
                                            rstd[:, w - 1, t:t + 1], ALU.subtract, ALU.mult)
                ins.then_inc(s_xn[w], 1)

            spike_ops = 3 * (STEPS - 1) + 1

            def spike_step(w, b, n, half=None):
                cols, made, base = slice(0, N), s_spk[w], (b - 1 if w == 1 else b) * spike_ops
                if half is not None:
                    cols = slice(half * N // 2, (half + 1) * N // 2)
                    made, base = s_spk_half[half], (0 if w == 1 else spike_ops)
                if n < 2:
                    dve.wait_ge(s_ysb[w], b * 2 + (1 if half == 0 else 2))
                else:
                    dve.wait_ge(made, base + (n if n % 3 != 1 else n - 1))
                mem, sign, fires = (ysb, 1.0, ALU.is_gt) if n < 3 else (negmem, -1.0, ALU.is_lt)
                if n == 0:
                    ins = dve.tensor_scalar(spikes[:, cols], mem[:, cols], THRESHOLD, None, fires)
                elif n % 3 == 0:
                    ins = dve.scalar_tensor_tensor(out=spikes[:, cols], in0=mem[:, cols], scalar=sign * THRESHOLD, in1=spikes[:, cols],
                                                   op0=fires, op1=ALU.add)
                elif n % 3 == 1:
                    ins = dve.scalar_tensor_tensor(out=drive[:, cols], in0=mem[:, cols], scalar=sign * BETA, in1=ysb[:, cols],
                                                   op0=ALU.mult, op1=ALU.add)
                else:
                    ins = dve.scalar_tensor_tensor(out=negmem[:, cols], in0=mem[:, cols], scalar=sign * THRESHOLD, in1=drive[:, cols],
                                                   op0=fires, op1=ALU.subtract)
                ins.then_inc(made, 1)

            def add_spikes(dst, src, w, b, done):
                dve.wait_ge(s_spk[w], (b if w == 1 else b + 1) * spike_ops)
                dve.scalar_tensor_tensor(out=dst, in0=spikes[:, :].rearrange("p (t c) -> p t c", c=C), scalar=0.5 / STEPS,
                                         in1=src, op0=ALU.mult, op1=ALU.add).then_inc(done, 1)

            def block_by_halves(dst, src, w, b, done):
                for n in range(spike_ops):
                    for half in range(2):
                        spike_step(w, b, n, half)
                for half in range(2):
                    tiles = slice(half * NT // 2, (half + 1) * NT // 2)
                    dve.wait_ge(s_spk_half[half], spike_ops * (1 if w == 1 else 2))
                    ins = dve.scalar_tensor_tensor(
                        out=dst[:, tiles, :], in0=spikes[:, half * N // 2:(half + 1) * N // 2].rearrange("p (t c) -> p t c", c=C),
                        scalar=0.5 / STEPS, in1=src[:, tiles, :], op0=ALU.mult, op1=ALU.add)
                ins.then_inc(done, 1)

            def finish1(b, par):
                add_spikes(x1[:, :, :], x_in[:, par, :, :], 1, b, s_x1)

            def stats2(b, par):
                dve.wait_ge(s_x1, b + 1)
                stats_of(2, x1, b)
                dve.tensor_tensor(x1b[:, par, :, :], x1[:, :, :],
                                  bias[:, :].rearrange("p (t c) -> p t c", t=1).to_broadcast([P, NT, C]), ALU.add).then_inc(s_x1b, 1)

            def residual2(src, t, b, par):
                dve.wait_ge(s_out, b * NT + (t + 1))
                if t == 0:
                    dve.wait_ge(s_x1b, b + 1)
                dve.tensor_tensor(x2[:, t, :], src[:, 0:C], x1b[:, par, t, :], ALU.add).then_inc(s_x2, 1)

            def stats3(b):
                dve.wait_ge(s_x2, b * NT + NT)
                stats_of(3, x2, b)

            def finish3(b):
                wait(dve, s_stored, b * 16)
                add_spikes(x3[:, :, :], x2[:, :, :], 3, b, s_x3)

            def low_half(n, kind, i, b, s, par):
                src = side_bank[n % 2][:, :]
                if kind == "q":
                    p = (s + 1) % PAIRS
                    dve.wait_ge(s_qhi, pair_no(b, p))
                    dve.tensor_tensor(q_lo[:, p % 2, 0, :], src, q_hi[:, p % 2, 0, :].bitcast(F32), ALU.subtract).then_inc(s_qlo, 1)
                elif kind == "k":
                    p = (s + 1) % PAIRS
                    dve.wait_ge(s_khi, pair_no(b, p))
                    bb, pp = before(b, p, 1)
                    for h in range(2):
                        wait(dve, s_keys[pp % 2][h], keys_no(bb, pp, h))
                    dve.tensor_tensor(k_lo[:, :], src, keys[:, p % 2, 0, :].bitcast(F32), ALU.subtract).then_inc(s_klo, 1)
                elif kind in ("t1", "t2", "t3"):
                    w = int(kind[1])
                    dve.wait_ge(s_xhi[w], b + 1)
                    hi, lo = (xa_hi[:, par, :], xa_lo[:, par, :]) if w == 2 else (xf_hi[:, :], xf_lo[:, :])
                    dve.tensor_tensor(lo, src, hi.bitcast(F32), ALU.subtract).then_inc(s_xlo[w], 1)
                elif kind == "out":
                    residual2(src, i, b, par)

            def steps(b, s, k, par, offsets):
                if 1 in offsets:
                    nb, npar = b + 1, 1 - par
                    if (s, k) == LN1["stats"]:
                        dve.wait_ge(s_xin[npar], (nb - npar) * 8 + 16)
                        stats_of(1, x_in[:, npar, :, :], nb)
                    if (s, k) == LN1["normalise"]:
                        normalise(1, x_in[:, npar, :, :], nb)
                    for n in range(spike_ops):
                        if (s, k) == SPIKE1[n]:
                            spike_step(1, nb, n)
                    if (s, k) == SPIKE1[spike_ops]:
                        finish1(nb, npar)
                    if (s, k) == LN2["stats"]:
                        stats2(nb, npar)
                    if (s, k) == LN2["normalise"]:
                        normalise(2, x1, nb)
                if -1 in offsets:
                    if (s, k) == LN3["stats"]:
                        stats3(b - 1)
                    if (s, k) == LN3["normalise"]:
                        normalise(3, x2, b - 1)
                    for n in range(spike_ops):
                        if (s, k) == SPIKE3[n]:
                            spike_step(3, b - 1, n)
                    if (s, k) == SPIKE3[spike_ops]:
                        finish3(b - 1)

            AGGREGATE = [(LN1["aggregate"], 1, 1), (LN3["aggregate"], 3, -1), (LN2["aggregate"], 2, 1)]

            def slot(b, s, par, offsets):
                for k in range(BEATS):
                    for at, w, off in AGGREGATE:
                        if at == (s, k) and off in offsets:
                            dve.wait_ge(s_stats[w], b + off + 1)
                    if exists(b, s):
                        bias_wait(b, s, k)
                    last = (b, s, k - 2) if k >= 2 else (*before(b, s, 1), BEATS + k - 2)
                    if exists(*last[:2]):
                        recip(*last)
                    if exists(b, s):
                        bias_max(b, s, k)
                    for at, w, off in AGGREGATE:
                        if at == (s, k) and off in offsets:
                            aggregate(w, b + off)
                    for n, kind, i, off, ss in side_at(s, k - 1, offsets):
                        low_half(n, kind, i, b + off, ss, (par + off) % 2)
                    steps(b, s, k, par, offsets)

            def number(kind, i=0):
                return [n for n, x in enumerate(SIDE) if x[2:4] == (kind, i)][0]

            def head():
                dve.wait_ge(s_xin[0], 16)
                stats_of(1, x_in[:, 0, :, :], 0)
                dve.wait_ge(s_stats[1], 1)
                aggregate(1, 0)
                dve.wait_ge(s_wfc_hi, 1)
                dve.tensor_tensor(wfc_lo[:, :], score_bank[0][:, :], wfc_hi[:, :].bitcast(F32), ALU.subtract).then_inc(s_wfc_lo, 1)
                normalise(1, x_in[:, 0, :, :], 0)
                low_half(number("t1"), "t1", 0, 0, 0, 0)
                dve.wait_ge(s_const, 3)
                for h in range(HEADS):
                    ins = dve.tensor_scalar(alibi[:, h, :], dist, SLOPES[h], None, ALU.mult)
                ins.then_inc(s_alibi, 1)
                for m, (hi, lo) in enumerate(((wq_hi, wq_lo), (wk_hi, wk_lo), (wv_hi, wv_lo))):
                    dve.wait_ge(s_whi, m + 1)
                    dve.scalar_tensor_tensor(out=lo[:, :], in0=w_raw[:, m * INNER:(m + 1) * INNER], scalar=-SCALE if m == 0 else 1.0,
                                             in1=hi[:, :].bitcast(F32), op0=ALU.mult, op1=ALU.subtract).then_inc(s_wlo, 1)
                block_by_halves(x1[:, :, :], x_in[:, 0, :, :], 1, 0, s_x1)
                dve.wait_ge(s_wo, 32)
                stats2(0, 0)
                dve.wait_ge(s_stats[2], 1)
                aggregate(2, 0)
                normalise(2, x1, 0)
                low_half(number("t2"), "t2", 0, 0, 0, 0)
                for n in range(len(SIDE) - 2, len(SIDE)):
                    low_half(n, SIDE[n][2], 0, 0, PAIRS - 1, 0)
                dve.wait_ge(s_alibi, 1)

            def tail():
                for s in range(2):
                    slot(B, s, B % 2, ())
                b = B - 1
                for t in range(NT):
                    residual2(last_out_bank[t], t, b, b % 2)
                stats3(b)
                dve.wait_ge(s_stats[3], b + 1)
                aggregate(3, b)
                normalise(3, x2, b)
                low_half(number("t3"), "t3", 0, b, 0, b % 2)
                wait(dve, s_stored, b * 16)
                block_by_halves(x3[:, :, :], x2[:, :, :], 3, b, s_x3)

            run(dve, slot, head, tail)

        @block.scalar
        def _(act):
            def exps(b, p, k):
                act.wait_ge(s_biased, tile_no(b, p, k))
                if k == 0:
                    bb, pp = before(b, p, 2)
                    wait(act, s_turned, turn_no(bb, pp, len(TRUNS) - 1))
                col = 0
                for h, i in TILES[k]:
                    seg = SEG[h, i]
                    ins = act.activation(prob[:, p % 2, h, PCOL[i]:PCOL[i] + WIDTH[i]], negsc[:, k % 3, col:col + WIDTH[i]],
                                         ACT.Exp, bias=negmax[:, p % 2, seg:seg + 1], scale=-1.0,
                                         accum_out=sums[:, p % 2, seg:seg + 1])
                    col += WIDTH[i]
                ins.then_inc(s_exp, 1)

            def turned_out(b, p, t):
                act.wait_ge(s_turned, turn_no(b, p, t))
                bb, pp = before(b, p, 2 if t < 3 else 1)
                wait(act, s_pv, pv_no(bb, pp, PVLAST[t + 2 if t < 3 else t - 3]))
                act.copy(probT[:, turn_slot(p, t), :], turn_bank[(len(TRUNS) * p + t) % 2][:, :]).then_inc(s_turned_out, 1)

            def att_out(b, p, par):
                act.wait_ge(s_pv, pv_no(b, p, NT - 1))
                if p == 2:
                    wait(act, s_out, b * NT)
                act.copy(attT[:, att_at(p, par), :], pv_bank[:, :]).then_inc(s_att, 1)

            def high_half(n, kind, i, b, s, par):
                src = side_bank[n % 2][:, :]
                if kind in "qk":
                    p = (s + 1) % PAIRS
                    dst, made, done = (q_hi, s_q, s_qhi) if kind == "q" else (keys, s_k, s_khi)
                    act.wait_ge(made, pair_no(b, p))
                    act.copy(dst[:, p % 2, 0, :], src).then_inc(done, 1)
                elif kind == "v":
                    q = s // 2
                    act.wait_ge(s_v, v_no(b, q, i))
                    wait(act, s_pv, pv_no(b, 2 * q - 3, NT - 1))
                    act.copy(vals[:, q % 2, 2 * i:2 * i + 2, :], src.rearrange("p (t n) -> p t n", t=2)).then_inc(s_vals, 1)
                elif kind in ("t1", "t2", "t3"):
                    w = int(kind[1])
                    act.wait_ge(s_xT[w], b + 1)
                    hi = xa_hi[:, par, :] if w == 2 else xf_hi[:, :]
                    if w == 1:
                        wait(act, s_fc[3], (b - 2) * FC)
                    if w == 3:
                        wait(act, s_fc[1], (b + 2) * FC + FC if not isinstance(b, int) else (min(b + 2, B - 1) + 1) * FC)
                    act.copy(hi, src).then_inc(s_xhi[w], 1)
                elif kind in ("fc1", "fc3"):
                    w = int(kind[2])
                    act.wait_ge(s_fc[w], b * FC + (i + 1))
                    if i == 0:
                        if w == 1:
                            wait(act, s_y[3], (b - 2) * 2)
                        else:
                            wait(act, s_y[1], (b + 3 if not isinstance(b, int) else min(b + 3, B)) * 2)
                    act.activation(hid[:, i, :], src, ACT.Relu).then_inc(s_relu[w], 1)
                elif kind in ("y1", "y3"):
                    w = int(kind[1])
                    act.wait_ge(s_y[w], b * 2 + (i + 1))
                    if w == 1:
                        wait(act, s_x3, b - 2)
                    else:
                        wait(act, s_x1, b + 3 if not isinstance(b, int) else min(b + 3, B))
                    act.copy(ysb[:, i * 2 * C:(i + 1) * 2 * C], src[:, 0:2 * C]).then_inc(s_ysb[w], 1)

            def slot(b, s, par, offsets):
                for k in range(BEATS):
                    for n, kind, i, off, ss in side_at(s, k - 1, offsets):
                        high_half(n, kind, i, b + off, ss, (par + off) % 2)
                    for t in range(len(TRUNS)):
                        if TBEAT[t] == k and exists(*before(b, s, 1)):
                            turned_out(*before(b, s, 1), t)
                    if k == ATTBEAT and exists(*before(b, s, 2)):
                        att_out(*before(b, s, 2), par if s >= 2 else 1 - par)
                    if exists(b, s):
                        exps(b, s, k)

            def chain(b, names):
                for n, (s, _, kind, i, off) in enumerate(SIDE):
                    if kind in names:
                        high_half(n, kind, i, b, s, b % 2)

            def head():
                act.wait_ge(s_wT, 1)
                act.copy(wfc_hi[:, :], score_bank[0][:, :]).then_inc(s_wfc_hi, 1)
                act.wait_ge(s_wT, 2)
                act.copy(wproj[:, :, :].rearrange("p t c -> p (t c)"), score_bank[1][:, :]).then_inc(s_wproj_out, 1)
                chain(0, ("t1", "fc1"))
                act.wait_ge(s_wqkv, 16)
                act.mul(wq_hi[:, :], w_raw[:, 0:INNER], -SCALE).then_inc(s_whi, 1)
                act.copy(wk_hi[:, :], w_raw[:, INNER:2 * INNER]).then_inc(s_whi, 1)
                act.copy(wv_hi[:, :], w_raw[:, 2 * INNER:3 * INNER]).then_inc(s_whi, 1)
                chain(0, ("y1", "t2"))
                for n in range(len(SIDE) - 2, len(SIDE)):
                    high_half(n, SIDE[n][2], 0, 0, PAIRS - 1, 0)
                act.wait_ge(s_wlo, 3)

            def tail():
                for s in range(2):
                    slot(B, s, B % 2, ())
                chain(B - 1, ("t3", "fc3", "y3"))

            run(act, slot, head, tail)

        @block.gpsimd
        def _(pool):
            def norm(b, p, k):
                pool.wait_ge(s_rsum, tile_no(b, p, k))
                for h, i in TILES[k]:
                    seg = SEG[h, i]
                    pr = prob[:, p % 2, h, PCOL[i]:PCOL[i] + WIDTH[i]]
                    ins = pool.tensor_tensor(pr, pr, rsum[:, p % 2, seg:seg + 1].to_broadcast([P, WIDTH[i]]), ALU.mult)
                ins.then_inc(s_norm, 1)

            def square(w, i, b):
                pool.wait_ge(s_relu[w], b * FC + (i + 1))
                pool.tensor_tensor(hid[:, i, :], hid[:, i, :], hid[:, i, :], ALU.mult).then_inc(s_hid[w], 1)

            def inverse_std(w, b):
                pool.wait_ge(s_mv[w], b + 1)
                pool.tensor_tensor(vareps[:, w - 1, :], meanvar[:, w - 1, :, 1], eps[:, :], ALU.add).then_inc(s_ve[w], 1)
                pool.wait_ge(s_ve[w], b + 1)
                pool.tensor_tensor(rstd[:, w - 1, :], vareps[:, w - 1, :], minus_half[:, :], ALU.pow).then_inc(s_rstd[w], 1)

            def slot(b, s, par, offsets):
                for k in range(BEATS):
                    for at, w, off in ((LN1["rstd"], 1, 1), (LN3["rstd"], 3, -1), (LN2["rstd"], 2, 1)):
                        if at == (s, k) and off in offsets:
                            inverse_std(w, b + off)
                    last = (b, s, k - 2) if k >= 2 else (*before(b, s, 1), BEATS + k - 2)
                    if exists(*last[:2]):
                        norm(*last)
                    for n, kind, i, off, _ in side_at(s, k - 1, offsets):
                        if kind in ("fc1", "fc3"):
                            square(int(kind[2]), i, b + off)

            def head():
                pool.memset(ident[:, :], 0.0).then_inc(s_const0, 1)
                pool.iota(dist, pattern=[[-1, N]], base=N - P, channel_multiplier=1,
                          allow_small_or_imprecise_dtypes=True).then_inc(s_dist0, 1)
                pool.memset(eps[:, :], EPS)
                pool.memset(minus_half[:, :], -0.5).then_inc(s_const, 1)
                pool.wait_ge(s_const0, 1)
                pool.affine_select(out=ident[:, :], in_=ident[:, :], compare_op=ALU.not_equal, fill=1.0, base=0,
                                   pattern=[[-1, P]], channel_multiplier=1).then_inc(s_const, 1)
                pool.wait_ge(s_dist0, 1)
                pool.affine_select(out=dist, in_=dist, compare_op=ALU.is_ge, fill=MASKED, base=N - P,
                                   pattern=[[-1, N]], channel_multiplier=1).then_inc(s_const, 1)
                pool.wait_ge(s_const, 1)
                inverse_std(1, 0)
                for i in range(FC):
                    square(1, i, 0)
                inverse_std(2, 0)

            def tail():
                for s in range(2):
                    slot(B, s, B % 2, ())
                inverse_std(3, B - 1)
                for i in range(FC):
                    square(3, i, B - 1)

            run(pool, slot, head, tail)


_INS = ['L0_attn_x', 'L0_attn_w_qkv', 'L0_attn_w_out', 'L0_attn_b_out', 'L0_ffn_W_fc', 'L0_ffn_W_proj']
_OUTS = [((16, 512, 128), 'float32')]


def kernel(**inputs):
    import numpy as _np
    import concourse.bacc as _bacc
    from concourse import mybir as _mybir
    from concourse.bass_utils import run_bass_kernel_spmd as _run

    nc = _bacc.Bacc("TRN2", target_bir_lowering=False, num_devices=1)
    arrays, args = {}, []
    for name in _INS:
        a = _np.ascontiguousarray(inputs[name])
        arrays[f"in_{name}_dram"] = a
        args.append(nc.dram_tensor(f"in_{name}_dram", a.shape, _mybir.dt.from_np(a.dtype), kind="ExternalInput").ap())
    for i, (shape, dtype) in enumerate(_OUTS):
        dt = _mybir.dt.from_np(_np.dtype(dtype))
        args.append(nc.dram_tensor(f"out_{i}_dram", shape, dt, kind="ExternalOutput").ap())
    macaron_kernel(nc, *args)
    r = _run(nc, [arrays], core_ids=[0])
    got = tuple(r.results[0][f"out_{i}_dram"] for i in range(len(_OUTS)))
    return got[0]
```
